# Optimizing a Trainium2 kernel written in Bass

```python
import numpy as np
import jax
import jax.numpy as jnp

def _softmax(x, axis=-1):
    return jax.nn.softmax(x, axis=axis)

def _gelu(x):
    return jax.nn.gelu(x, approximate=True)

def _silu(x):
    return jax.nn.silu(x)

def _sigmoid(x):
    return jax.nn.sigmoid(x)

def _layernorm(x, axis=-1, eps=1e-05):
    m = jnp.mean(x, axis=axis, keepdims=True)
    v = jnp.var(x, axis=axis, keepdims=True)
    return (x - m) / jnp.sqrt(v + eps)

def _scatter_add(tgt, idx, src, axis=0):
    return tgt.at[idx].add(src)

def _segment_sum(src, seg, n):
    return jax.ops.segment_sum(src, seg, n)
kernel_name = 'mk_gnn_resnorm_d2_gnn_r32_46bda9'

def setup_inputs(seed: int=0):
    np.random.seed(seed)
    _w = jnp.asarray

    def _rec_inputs():
        import jax
        import jax.numpy as jnp
        _gk = jax.random.key(seed)
        x = -0.000202 + 1 * jax.random.normal(jax.random.fold_in(_gk, 1), (3125, 64), jnp.float32)
        _s = jax.random.randint(jax.random.fold_in(_gk, 2), (25000,), 0, 3125, jnp.int32)
        _d = jax.random.randint(jax.random.fold_in(_gk, 3), (25000,), 0, 3125, jnp.int32)
        _loop = jnp.arange(3125, dtype=jnp.int32)
        src = jnp.concatenate([_s, _d, _loop])
        dst = jnp.concatenate([_d, _s, _loop])
        _o = jnp.argsort(dst, stable=True)
        src = src[_o]
        dst = dst[_o]
        edge_attr_64 = -9.77346e-05 + 0.999888 * jax.random.normal(jax.random.fold_in(_gk, 11), (53125, 64), jnp.float32)
        return (x, src, dst, edge_attr_64)
    x, src, dst, edge_attr_64 = _rec_inputs()

    def _L0_gnn_setup():
        import jax, jax.numpy as jnp
        import numpy as np
        N_NODES = 3125
        N_EDGES = 25000
        DIM = 64
        NUM_HEADS = 4
        HEAD_DIM = DIM // NUM_HEADS
        key = jax.random.key(seed)
        ks = jax.random.split(key, 7)
        w_scale = 1.0 / np.sqrt(DIM)
        x = jax.random.normal(ks[0], (N_NODES, DIM), dtype=jnp.float32)
        edge_attr = jax.random.normal(ks[1], (N_EDGES, DIM), dtype=jnp.float32)
        edge_index = jax.random.randint(ks[2], (2, N_EDGES), 0, N_NODES, dtype=jnp.int64)
        Wq = jax.random.normal(ks[3], (DIM, DIM), dtype=jnp.float32) * w_scale
        Wk = jax.random.normal(ks[4], (DIM, DIM), dtype=jnp.float32) * w_scale
        We = jax.random.normal(ks[5], (DIM, DIM), dtype=jnp.float32) * w_scale
        Wv = jax.random.normal(ks[6], (DIM, DIM), dtype=jnp.float32) * w_scale
        return {'x': x, 'edge_attr': edge_attr, 'Wq': Wq, 'Wk': Wk, 'We': We, 'Wv': Wv, 'edge_index': edge_index}
    _L0_gnn_all = _L0_gnn_setup()
    _L0_gnn_in = {k: v for k, v in _L0_gnn_all.items() if k in ('Wq', 'Wk', 'We', 'Wv')}
    del _L0_gnn_all

    def _L1_gnn_setup():
        import jax, jax.numpy as jnp
        import numpy as np
        N_NODES = 3125
        N_EDGES = 50000
        IN_FEAT = 64
        HIDDEN = 64

        def _sage_conv(h, src, dst, W_l, b, W_r):
            n = h.shape[0]
            msg = h[src]
            agg = jax.ops.segment_sum(msg, dst, num_segments=n)
            cnt = jax.ops.segment_sum(jnp.ones((src.shape[0],), h.dtype), dst, num_segments=n)
            mean = agg / jnp.maximum(cnt, 1.0)[:, None]
            return mean @ W_l.T + b + h @ W_r.T
        key = jax.random.key(seed)
        ks = jax.random.split(key, 8)
        s = 0.05
        x = jax.random.normal(ks[0], (N_NODES, IN_FEAT), dtype=jnp.float32)
        edge_index = jax.random.randint(ks[1], (2, N_EDGES), 0, N_NODES, dtype=jnp.int64)
        return {'x': x, 'edge_index': edge_index, 'W_l1': jax.random.normal(ks[2], (HIDDEN, IN_FEAT), dtype=jnp.float32) * s, 'b1': jnp.zeros((HIDDEN,), dtype=jnp.float32), 'W_r1': jax.random.normal(ks[3], (HIDDEN, IN_FEAT), dtype=jnp.float32) * s, 'W_l2': jax.random.normal(ks[4], (HIDDEN, HIDDEN), dtype=jnp.float32) * s, 'b2': jnp.zeros((HIDDEN,), dtype=jnp.float32), 'W_r2': jax.random.normal(ks[5], (HIDDEN, HIDDEN), dtype=jnp.float32) * s}
    _L1_gnn_all = _L1_gnn_setup()
    _L1_gnn_in = {k: v for k, v in _L1_gnn_all.items() if k in ('W_l1', 'b1', 'W_r1', 'W_l2', 'b2', 'W_r2')}
    del _L1_gnn_all
    return {'x': x, 'src': src, 'dst': dst, 'edge_attr_64': edge_attr_64, 'L0_gnn_Wq': _L0_gnn_in['Wq'], 'L0_gnn_Wk': _L0_gnn_in['Wk'], 'L0_gnn_We': _L0_gnn_in['We'], 'L0_gnn_Wv': _L0_gnn_in['Wv'], 'L1_gnn_W_l1': _L1_gnn_in['W_l1'], 'L1_gnn_b1': _L1_gnn_in['b1'], 'L1_gnn_W_r1': _L1_gnn_in['W_r1'], 'L1_gnn_W_l2': _L1_gnn_in['W_l2'], 'L1_gnn_b2': _L1_gnn_in['b2'], 'L1_gnn_W_r2': _L1_gnn_in['W_r2']}

def reference(x, src, dst, edge_attr_64, L0_gnn_Wq, L0_gnn_Wk, L0_gnn_We, L0_gnn_Wv, L1_gnn_W_l1, L1_gnn_b1, L1_gnn_W_r1, L1_gnn_W_l2, L1_gnn_b2, L1_gnn_W_r2):
    import jax
    import jax.numpy as jnp

    def _L0_gnn_ref(x, edge_attr, Wq, Wk, We, Wv, edge_index):
        import jax, jax.numpy as jnp
        import numpy as np
        N_NODES = 3125
        N_EDGES = 25000
        DIM = 64
        NUM_HEADS = 4
        HEAD_DIM = DIM // NUM_HEADS
        n = x.shape[0]
        Q_h = (x @ Wq.T).reshape(n, NUM_HEADS, HEAD_DIM)
        K_h = (x @ Wk.T).reshape(n, NUM_HEADS, HEAD_DIM)
        V_h = (x @ Wv.T).reshape(n, NUM_HEADS, HEAD_DIM)
        E = (edge_attr @ We.T).reshape(-1, NUM_HEADS, HEAD_DIM)
        src_idx = edge_index[0]
        dst_idx = edge_index[1]
        src = K_h[src_idx]
        dest = Q_h[dst_idx]
        score = src * dest / np.sqrt(HEAD_DIM).astype(np.float32)
        score = score * E
        score = jnp.exp(jnp.clip(score.sum(-1, keepdims=True), -5.0, 5.0))
        msg = V_h[src_idx] * score
        wV = jax.ops.segment_sum(msg, dst_idx, num_segments=n)
        Z = jax.ops.segment_sum(score, dst_idx, num_segments=n)
        h_out = wV / (Z + 1e-06)
        return h_out.reshape(n, NUM_HEADS * HEAD_DIM)

    def _L1_gnn_ref(x, edge_index, W_l1, b1, W_r1, W_l2, b2, W_r2):
        import jax, jax.numpy as jnp
        import numpy as np
        N_NODES = 3125
        N_EDGES = 50000
        IN_FEAT = 64
        HIDDEN = 64

        def _sage_conv(h, src, dst, W_l, b, W_r):
            n = h.shape[0]
            msg = h[src]
            agg = jax.ops.segment_sum(msg, dst, num_segments=n)
            cnt = jax.ops.segment_sum(jnp.ones((src.shape[0],), h.dtype), dst, num_segments=n)
            mean = agg / jnp.maximum(cnt, 1.0)[:, None]
            return mean @ W_l.T + b + h @ W_r.T
        src, dst = (edge_index[0], edge_index[1])
        h = jax.nn.relu(_sage_conv(x, src, dst, W_l1, b1, W_r1))
        return jax.nn.relu(_sage_conv(h, src, dst, W_l2, b2, W_r2))
    edge_index = jnp.stack([src, dst])
    x = _layernorm(x + _L0_gnn_ref(x, edge_attr_64, L0_gnn_Wq, L0_gnn_Wk, L0_gnn_We, L0_gnn_Wv, edge_index), axis=-1)
    x = _layernorm(x + _L1_gnn_ref(x, edge_index, L1_gnn_W_l1, L1_gnn_b1, L1_gnn_W_r1, L1_gnn_W_l2, L1_gnn_b2, L1_gnn_W_r2), axis=-1)
    return x

_drawn_inputs = setup_inputs


def setup_inputs(seed=0):
    import zlib

    import numpy as np

    out = dict(_drawn_inputs(seed))
    spreads = {'L1_gnn_b1': (0.0, 0.373), 'L1_gnn_b2': (0.0, 0.1)}
    factors = {'L1_gnn_W_l1': 2.925}
    for name, (base, spread) in spreads.items():
        noise = np.random.default_rng([zlib.crc32(name.encode()), seed]).standard_normal(out[name].shape)
        drawn = base * np.exp(spread * noise) if base else spread * noise
        out[name] = jnp.asarray(drawn.astype(out[name].dtype))
    for name, factor in factors.items():
        out[name] = (out[name] * factor).astype(out[name].dtype)
    return out
```

```python
import concourse.bass as bass
from concourse import mybir
from contextlib import ExitStack


def gnn_kernel(nc, x, src, dst, edge_attr, Wq, Wk, We, Wv, Wl1, b1, Wr1, Wl2, b2, Wr2, out):
    f32, bf16, f16, i32 = mybir.dt.float32, mybir.dt.bfloat16, mybir.dt.float16, mybir.dt.int32
    ALU = mybir.AluOpType
    ACT = mybir.ActivationFunctionType
    X = mybir.AxisListType.X

    N, F = x.shape
    E = src.shape[0]
    HEADS = 4
    HD = F // HEADS
    P = 128
    NB = 25
    NP = N // NB
    T = 4
    GE = P * T
    NG = -(-E // GE)
    TAIL = E - (NG - 1) * GE
    TFULL, TREST = TAIL // T, TAIL % T
    W = 40
    WH = W // 2
    KEYS = W * NB
    NW = N + W
    MSG = F + HEADS + 1
    FAR = 1 << 20
    DUP = 127
    MAGIC = 1.5 * 2.0 ** 23
    EPS = 1e-5
    BB = 4

    ctx = ExitStack()
    with ctx:
        def sb(stack, name, shape, dt=f32, side="left"):
            return stack.enter_context(nc.sbuf_tensor(name, shape, dt, side=side))

        def pb(stack, name, shape):
            return stack.enter_context(nc.psum_tensor(name, shape, f32))

        def sem(name):
            return ctx.enter_context(nc.semaphore(name))

        kv_table = nc.dram_tensor("kv_table", (N, 2 * F), f32, kind="Internal").ap()
        q_table = nc.dram_tensor("q_table", (NW, F), f32, kind="Internal").ap()

        ident = sb(ctx, "ident", [P, P])
        x_sb = sb(ctx, "x_sb", [NP, NB, F])
        wl_wr_T = sb(ctx, "wl_wr_T", [F, 2, 2 * F])
        bias = sb(ctx, "bias", [P, 2, F])
        sums_T = sb(ctx, "sums_T", [MSG, NW])

        s_load, s_wload, s_xload, s_idx = sem("rows_loaded"), sem("weights_loaded"), sem("x_loaded"), sem("bias_loaded")
        s_pad = sem("padding_written")
        s_id = sem("identity_ready")
        s_rowsf = sem("rows_converted")
        s_idT = sem("index_transposed")
        s_base = sem("base_row_ready")
        s_bb = sem("base_broadcast")
        s_tab = sem("table_chain")
        s_tabs = sem("tables_ready")
        s_iota = sem("iota_ready")
        s_wT, s_wc = sem("weights_transposed"), sem("weights_copied")
        s_xT, s_xc = sem("x_transposed"), sem("x_copied")
        s_proj, s_projc = sem("projected"), sem("projection_copied")
        s_tstore = sem("tables_stored")
        s_zero = sem("zeros_ready")

        edge_ctx = ExitStack()
        src_i = sb(edge_ctx, "src_i", [P, NG, T], i32)
        lo_tab = sb(edge_ctx, "lo_tab", [P, NG, T], f16)
        key_tab = sb(edge_ctx, "key_tab", [P, NG, T], f16)
        rel_tab = sb(edge_ctx, "rel_tab", [P, NG, T])
        base_i = sb(edge_ctx, "base_i", [1, NG], i32)
        iota = sb(edge_ctx, "iota", [P, KEYS], f16)
        we_diag = sb(edge_ctx, "we_diag", [P, P])

        tab_ctx = ExitStack()
        rows_i = sb(tab_ctx, "rows_i", [NG, 2, GE], i32, side="right")
        rows_f = sb(tab_ctx, "rows_f", [NG, 2, GE], side="right")
        src_f = sb(tab_ctx, "src_f", [P, NG, T], side="right")
        dst_f = sb(tab_ctx, "dst_f", [P, NG, T], side="right")
        hi_tab = sb(tab_ctx, "hi_tab", [P, NG, T], side="right")
        in_tab = sb(tab_ctx, "in_tab", [P, NG, T], side="right")
        iota_i = sb(tab_ctx, "iota_i", [P, KEYS], i32, side="right")
        ones_row = sb(tab_ctx, "ones_row", [1, P], side="right")
        w_kv = sb(tab_ctx, "w_kv", [2 * F, F], side="right")
        w_q = sb(tab_ctx, "w_q", [F, F], side="right")
        w_ee = sb(tab_ctx, "w_ee", [F, 2, F], side="right")
        w_s = sb(tab_ctx, "w_s", [2 * F, 2, F], side="right")
        w_kvq_T = sb(tab_ctx, "w_kvq_T", [F, 3 * F], side="right")
        x_T = sb(tab_ctx, "x_T", [F, N], side="right")
        kvq = sb(tab_ctx, "kvq", [NP, NB, 3 * F], side="right")
        zeros = sb(tab_ctx, "zeros", [W, F], side="right")

        ps_s = pb(tab_ctx, "ps_s", [P, 512])
        ps_d = pb(tab_ctx, "ps_d", [P, 512])
        ps_b = pb(tab_ctx, "ps_b", [P, 512])
        ps_w = pb(tab_ctx, "ps_w", [P, 512])
        ps_x = pb(tab_ctx, "ps_x", [P, 2, 512])
        ps_k = pb(tab_ctx, "ps_k", [P, 2, 512])
        XG = -(-NB // BB)

        with nc.Block() as block:
            @block.sync
            def _(sp):
                sp.dma_start(x_sb[:, :, :], x.rearrange("(b p) f -> p b f", p=NP)).then_inc(s_xload, 16)
                sp.dma_start(w_kv[0:F, :], Wk).then_inc(s_wload, 16)
                sp.dma_start(w_kv[F:, :], Wv).then_inc(s_wload, 16)
                sp.dma_start(w_q[:, :], Wq).then_inc(s_wload, 16)
                for c in range(2):
                    sp.dma_start(w_ee[:, c, :], We).then_inc(s_wload, 16)
                for c, (wl, wr) in enumerate([(Wl1, Wr1), (Wl2, Wr2)]):
                    sp.dma_start(w_s[0:F, c, :], wl).then_inc(s_wload, 16)
                    sp.dma_start(w_s[F:, c, :], wr).then_inc(s_wload, 16)
                for c, b in enumerate((b1, b2)):
                    sp.dma_start(bias[:, c, :], b.rearrange("(a f) -> a f", a=1).to_broadcast([P, F])).then_inc(s_idx, 16)
                sp.wait_ge(s_zero, 1)
                sp.dma_start(q_table[N:NW, :], zeros[:, :]).then_inc(s_tstore, 16)
                for r in range(0, NB, 8):
                    k = min(8, NB - r)
                    sp.wait_ge(s_projc, min(r + 8, NB))
                    sp.dma_start(kv_table.rearrange("(b p) f -> p b f", p=NP)[:, r:r + k, :],
                                 kvq[:, r:r + k, 0:2 * F]).then_inc(s_tstore, 16)
                    sp.dma_start(q_table[0:N, :].rearrange("(b p) f -> p b f", p=NP)[:, r:r + k, :],
                                 kvq[:, r:r + k, 2 * F:]).then_inc(s_tstore, 16)
                sp.wait_ge(s_idx, 32)
                sp.wait_ge(s_tstore, 16 * (1 + 2 * (-(-NB // 8))))

            @block.scalar
            def _(act):
                act.wait_ge(s_pad, 2)
                for c, a in enumerate((src, dst)):
                    act.dma_start(rows_i[0:NG - 1, c, :],
                                  a[0:(NG - 1) * GE].rearrange("(g e) -> g e", e=GE)).then_inc(s_load, 16)
                    act.dma_start(rows_i[NG - 1:NG, c, 0:TAIL],
                                  a[(NG - 1) * GE:E].rearrange("(g e) -> g e", g=1)).then_inc(s_load, 16)
                for r in range(XG):
                    n = min(BB, NB - BB * r) * NP
                    act.wait_ge(s_xT, r + 1)
                    nc.scalar.activation(x_T[:, BB * r * NP:BB * r * NP + n], ps_x[0:F, r % 2, 0:n],
                                         ACT.Copy).then_inc(s_xc, 1)

            @block.gpsimd
            def _(pool):
                nc.gpsimd.memset(rows_i[:, 0, :], 0).then_inc(s_pad, 1)
                nc.gpsimd.memset(rows_i[:, 1, :], FAR).then_inc(s_pad, 1)
                nc.gpsimd.memset(zeros[:, :], 0.0).then_inc(s_zero, 1)
                nc.gpsimd.memset(ident[:, :], 0.0).then_inc(s_id, 1)
                nc.gpsimd.memset(ones_row[:, :], 1.0).then_inc(s_id, 1)
                pool.wait_ge(s_id, 2)
                nc.gpsimd.affine_select(out=ident[:, :], in_=ident[:, :], compare_op=ALU.not_equal, fill=1.0,
                                        base=0, pattern=[[-1, P]], channel_multiplier=1).then_inc(s_id, 1)
                nc.gpsimd.iota(iota_i[:, :], [[1, KEYS]], base=0, channel_multiplier=0).then_inc(s_iota, 1)
                nc.gpsimd.memset(sums_T[:, :], 0.0).then_inc(s_zero, 1)
                nc.gpsimd.memset(we_diag[:, :], 0.0).then_inc(s_zero, 1)

            @block.tensor
            def _(pe):
                pe.wait_ge(s_id, 3)
                pe.wait_ge(s_wload, 16 * 9)
                nc.tensor.transpose(ps_w[0:F, 0:P], w_kv[:, :], ident[:, :])
                nc.tensor.transpose(ps_w[0:F, P:P + F], w_q[:, :], ident[0:F, 0:F])
                nc.tensor.transpose(ps_w[:, P + F:2 * P], w_ee[:, :, :].rearrange("p a f -> p (a f)"), ident[0:F, 0:F])
                nc.tensor.transpose(ps_w[0:F, 2 * P:3 * P], w_s[:, 0, :], ident[:, :])
                nc.tensor.transpose(ps_w[0:F, 3 * P:4 * P], w_s[:, 1, :], ident[:, :]).then_inc(s_wT, 1)
                pe.wait_ge(s_xload, 16)

                def project(r):
                    pe.wait_ge(s_xc, r + 1)
                    for b in range(BB * r, min(BB * r + BB, NB)):
                        if b >= 4 and b % 2 == 0:
                            pe.wait_ge(s_projc, b - 2)
                        nc.tensor.matmul(ps_k[0:NP, b // 2 % 2, b % 2 * 3 * F:(b % 2 + 1) * 3 * F],
                                         x_T[:, b * NP:(b + 1) * NP], w_kvq_T[:, :],
                                         start=True, stop=True).then_inc(s_proj, 1)

                for r in range(XG):
                    if r >= 2:
                        pe.wait_ge(s_xc, r - 1)
                    for b in range(BB * r, min(BB * r + BB, NB)):
                        t = nc.tensor.transpose(ps_x[0:F, r % 2, (b - BB * r) * NP:(b - BB * r + 1) * NP],
                                                x_sb[:, b, :], ident[0:NP, 0:NP])
                    t.then_inc(s_xT, 1)
                    if r == 0:
                        pe.wait_ge(s_rowsf, 2)
                        for c, ps in enumerate((ps_s, ps_d)):
                            for j in range(T):
                                nc.tensor.transpose(ps[:, j * NG:(j + 1) * NG], rows_f[:, c, j::T],
                                                    ident[0:NG, 0:NG]).then_inc(s_idT, 1)
                        pe.wait_ge(s_wc, 2)
                        pe.wait_ge(s_base, 1)
                        nc.tensor.matmul(ps_b[:, 0:NG], ones_row[:, :], dst_f[0:1, :, 0],
                                         start=True, stop=True).then_inc(s_bb, 1)
                    else:
                        project(r - 1)
                project(XG - 1)

            @block.vector
            def _(dve):
                steps = [0]

                def after(ins):
                    steps[0] += 1
                    ins.then_inc(s_tab, 1)
                    dve.wait_ge(s_tab, steps[0])

                dve.wait_ge(s_load, 64)
                for c in range(2):
                    nc.vector.tensor_copy(rows_f[:, c, :], rows_i[:, c, :]).then_inc(s_rowsf, 1)
                dve.wait_ge(s_wT, 1)
                dve.wait_ge(s_zero, 3)
                nc.vector.tensor_copy(w_kvq_T[:, :], ps_w[0:F, 0:3 * F]).then_inc(s_wc, 1)
                nc.vector.tensor_copy(wl_wr_T[:, :, :].rearrange("p a f -> p (a f)"), ps_w[0:F, 2 * P:4 * P])
                nc.vector.tensor_copy(we_diag[0:F, 0:F], ps_w[0:F, P + F:2 * P])
                nc.vector.tensor_copy(we_diag[F:, F:], ps_w[F:, P + F:2 * P]).then_inc(s_wc, 1)
                dve.wait_ge(s_idT, T)
                after(nc.vector.tensor_copy(src_f[:, :, :], ps_s[:, 0:T * NG].rearrange("p (j g) -> p g j", j=T)))
                nc.vector.tensor_copy(src_i[:, :, :], src_f[:, :, :])
                dve.wait_ge(s_idT, 2 * T)
                nc.vector.tensor_copy(dst_f[:, :, :], ps_d[:, 0:T * NG].rearrange("p (j g) -> p g j", j=T)).then_inc(s_base, 1)
                dve.wait_ge(s_base, 1)
                nc.vector.tensor_copy(base_i[:, :], dst_f[0:1, :, 0])

                def evacuate(b):
                    dve.wait_ge(s_proj, min(b // 2 * 2 + 2, NB))
                    nc.vector.tensor_copy(kvq[:, b, :], ps_k[0:NP, b // 2 % 2, b % 2 * 3 * F:(b % 2 + 1) * 3 * F]).then_inc(s_projc, 1)

                after(nc.vector.tensor_scalar(hi_tab[:, :, :], src_f[:, :, :], 1.0 / NP, -(NP // 2) / NP, ALU.mult, ALU.add))
                after(nc.vector.tensor_scalar(hi_tab[:, :, :], hi_tab[:, :, :], MAGIC, -MAGIC, ALU.add, ALU.add))
                nc.vector.scalar_tensor_tensor(out=lo_tab[:, :, :], in0=hi_tab[:, :, :], scalar=-float(NP),
                                               in1=src_f[:, :, :], op0=ALU.mult, op1=ALU.add)
                dve.wait_ge(s_bb, 1)
                after(nc.vector.tensor_tensor(rel_tab[:, :, :], dst_f[:, :, :],
                                              ps_b[:, 0:NG].rearrange("p (g a) -> p g a", a=1).to_broadcast([P, NG, T]), ALU.subtract))
                nc.vector.scalar_tensor_tensor(out=hi_tab[:, :, :], in0=rel_tab[:, :, :], scalar=float(NB),
                                               in1=hi_tab[:, :, :], op0=ALU.mult, op1=ALU.add)
                after(nc.vector.tensor_scalar(in_tab[:, :, :], rel_tab[:, :, :], float(W), None, ALU.is_lt))
                after(nc.vector.scalar_tensor_tensor(out=hi_tab[:, :, :], in0=hi_tab[:, :, :], scalar=1.0,
                                                     in1=in_tab[:, :, :], op0=ALU.add, op1=ALU.mult))
                nc.vector.tensor_scalar(key_tab[:, :, :], hi_tab[:, :, :], -1.0, None, ALU.add)
                dve.wait_ge(s_iota, 1)
                nc.vector.tensor_copy(iota[:, :], iota_i[:, :])
                for b in range(NB):
                    evacuate(b)

        tab_ctx.close()
        counts_ctx = ExitStack()
        counts_T = sb(counts_ctx, "counts_T", [P, NB, NW], bf16, side="right")

        e_ctx = ExitStack()
        SL = 2
        src_now = sb(e_ctx, "src_now", [P, SL, T], i32)
        kv = sb(e_ctx, "kv", [P, SL, T, 2 * F])
        ea = sb(e_ctx, "ea", [P, SL, T, F])
        q_win = sb(e_ctx, "q_win", [W, SL, F])
        d_hot = sb(e_ctx, "d_hot", [P, SL, T, W])
        d_hot_T = sb(e_ctx, "d_hot_T", [W, T, P])
        ea_T = sb(e_ctx, "ea_T", [P, T // 2, P])
        l_hot = sb(e_ctx, "l_hot", [P, T, P], bf16)
        k_hot = sb(e_ctx, "k_hot", [P, T, KEYS], bf16)
        kq = sb(e_ctx, "kq", [P, T, F])
        kqe = sb(e_ctx, "kqe", [P, T, F])
        score = sb(e_ctx, "score", [P, T * HEADS])
        score_c = sb(e_ctx, "score_c", [P, T, HEADS])
        msg = sb(e_ctx, "msg", [P, SL, T, MSG])

        ps_dT = pb(e_ctx, "ps_dT", [P, 512])
        ps_eT = pb(e_ctx, "ps_eT", [P, 512])
        ps_eq = pb(e_ctx, "ps_eq", [P, 2, T, F])
        ps_sum = pb(e_ctx, "ps_sum", [P, 512])
        ps_cnt = pb(e_ctx, "ps_cnt", [P, SL, 2, 512])

        ea_arrived = [sem(f"ea_arrived{s}") for s in range(SL)]
        q_arrived = [sem(f"q_arrived{s}") for s in range(SL)]
        kv_arrived = [sem(f"kv_arrived{s}") for s in range(SL)]
        src_ready = sem("src_ready")
        ones_ready = sem("ones_ready")
        gathers_begun = sem("gathers_begun")
        edges_zeroed = sem("edges_zeroed")
        transposed = sem("transposed")
        t_copied = sem("t_copied")
        eq_ready = sem("eq_ready")
        eq_used = sem("eq_used")
        kq_done = sem("kq_done")
        heads_done = sem("heads_done")
        clip_ready = sem("clip_ready")
        exp_ready = sem("exp_ready")
        msg_ready = sem("msg_ready")
        d_ready = sem("d_ready")
        hot_ready = sem("hot_ready")
        cnt_done = sem("cnt_done")
        cnt_copied = sem("cnt_copied")
        col_added = sem("col_added")
        sum_done = sem("sum_done")
        sum_added = sem("sum_added")

        ITER = NG // SL

        def steps(eng, body):
            for s in range(SL):
                body(0, s)
            with eng.Fori(1, ITER - 1) as i:
                for s in range(SL):
                    body(i, s)
            for s in range(SL):
                body(ITER - 1, s)

        def at(i, s, ahead):
            return i + (s + ahead) // SL, (s + ahead) % SL

        def exists(i, s, ahead):
            return not (isinstance(i, int) and not 0 <= SL * i + s + ahead < NG)

        with nc.Block() as block:
            @block.sync
            def _(sp):
                def body(i, s):
                    g = SL * i + s
                    if exists(i, s, -SL):
                        sp.wait_ge(transposed, g - 1)
                    if isinstance(i, int) and g == NG - 1:
                        sp.dma_start(ea[0:TFULL, s, :, :],
                                     edge_attr[g * GE:g * GE + TFULL * T, :].rearrange("(p j) f -> p j f", j=T)).then_inc(ea_arrived[s], 16)
                        sp.dma_start(ea[TFULL:TFULL + 1, s, 0:TREST, :],
                                     edge_attr[g * GE + TFULL * T:E, :].rearrange("(p j) f -> p j f", p=1)).then_inc(ea_arrived[s], 16)
                    else:
                        sp.dma_start(ea[:, s, :, :],
                                     edge_attr[bass.ds(g * GE, GE), :].rearrange("(p j) f -> p j f", j=T)).then_inc(ea_arrived[s], 16)
                    if exists(i, s, -SL):
                        sp.wait_ge(eq_ready, g - 1)
                    base = sp.value_load(base_i[0:1, bass.ds(g, 1)], min_val=0, max_val=N - 1)
                    sp.dma_start(q_win[:, s, :], q_table[bass.ds(base, W), :]).then_inc(q_arrived[s], 16)
                steps(sp, body)

            @block.gpsimd
            def _(pool):
                nc.gpsimd.memset(counts_T[:, :, 0:1], 0.0).then_inc(edges_zeroed, 1)
                nc.gpsimd.memset(counts_T[:, :, N:NW], 0.0).then_inc(edges_zeroed, 1)

                def body(i, s):
                    g = SL * i + s
                    pool.wait_ge(src_ready, g + 1)
                    if exists(i, s, -SL):
                        pool.wait_ge(msg_ready, g - 1)
                    pool.sem_inc(gathers_begun, 1)
                    for j in range(T):
                        nc.gpsimd.indirect_dma_start(kv[:, s, j, :], None, kv_table[:, :],
                                                     bass.IndirectOffsetOnAxis(ap=src_now[:, s, j:j + 1], axis=0)
                                                     ).then_inc(kv_arrived[s], 16)
                steps(pool, body)

            @block.scalar
            def _(act):
                def take_sources(i, s):
                    g = SL * i + s
                    nc.scalar.activation(src_now[:, s, :], src_i[:, bass.ds(g, 1), :].rearrange("p a j -> p (a j)"),
                                         ACT.Copy).then_inc(src_ready, 1)

                def copy_transposed(i, s):
                    g = SL * i + s
                    act.wait_ge(transposed, g + 1)
                    if exists(i, s, -1):
                        act.wait_ge(eq_ready, g)
                    nc.scalar.activation(d_hot_T[:, :, :].rearrange("p j e -> p (j e)"), ps_dT[0:W, :], ACT.Copy)
                    nc.scalar.activation(ea_T[:, :, :].rearrange("p j e -> p (j e)"), ps_eT[:, 0:T // 2 * P],
                                         ACT.Copy).then_inc(t_copied, 1)

                for s in range(SL):
                    take_sources(0, s)
                copy_transposed(0, 0)
                act.wait_ge(edges_zeroed, 2)

                def body(i, s):
                    g = SL * i + s
                    act.wait_ge(clip_ready, g + 1)
                    nc.scalar.activation(msg[:, s, :, F:F + HEADS], score_c[:, :, :], ACT.Exp,
                                         scale=1.0 / HD ** 0.5).then_inc(exp_ready, 1)
                    if exists(i, s, SL):
                        act.wait_ge(kv_arrived[s], 16 * T * (i + 1))
                        take_sources(i + 1, s)
                    if exists(i, s, 1):
                        copy_transposed(*at(i, s, 1))
                    base = act.value_load(base_i[0:1, bass.ds(g, 1)], min_val=0, max_val=N - 1)
                    act.wait_ge(cnt_done, T * (g + 1))
                    if exists(i, s, -1):
                        act.wait_ge(col_added, g)
                    for h in range(2):
                        d0 = 1 - h
                        last = nc.scalar.activation(
                            counts_T[:, :, bass.ds(base + (h * WH + d0), WH - d0)],
                            ps_cnt[:, s, h, d0 * NB:WH * NB].rearrange("p (d b) -> p b d", b=NB), ACT.Copy)
                    last.then_inc(cnt_copied, 1)
                steps(act, body)

            @block.vector
            def _(dve):
                def targets(i, s):
                    g = SL * i + s
                    for j in range(T):
                        last = nc.vector.tensor_scalar(d_hot[:, s, j, :], iota[:, 0:W],
                                                       rel_tab[:, bass.ds(g, 1), j:j + 1].rearrange("p a j -> p (a j)"),
                                                       None, ALU.is_equal)
                    last.then_inc(d_ready, 1)

                def one_hots(i, s):
                    g = SL * i + s
                    for j in range(T):
                        if exists(i, s, -1):
                            dve.wait_ge(cnt_done, T * g - T + j + 1)
                        nc.vector.tensor_scalar(l_hot[:, j, :], iota[:, 0:P],
                                                lo_tab[:, bass.ds(g, 1), j:j + 1].rearrange("p a j -> p (a j)"), None, ALU.is_equal)
                        nc.vector.tensor_scalar(k_hot[:, j, :], iota[:, :],
                                                key_tab[:, bass.ds(g, 1), j:j + 1].rearrange("p a j -> p (a j)"),
                                                None, ALU.is_equal).then_inc(hot_ready, 1)

                def add_sums(i, s):
                    g = SL * i + s
                    base = dve.value_load(base_i[0:1, bass.ds(g, 1)], min_val=0, max_val=N - 1)
                    dve.wait_ge(sum_done, g + 1)
                    if exists(i, s, -1):
                        dve.wait_ge(sum_added, g)
                    window = sums_T[:, bass.ds(base, W)]
                    nc.vector.tensor_tensor(window, window, ps_sum[0:MSG, 0:W], ALU.add).then_inc(sum_added, 1)
                    dve.wait_ge(cnt_copied, g + 1)
                    if exists(i, s, -1):
                        dve.wait_ge(col_added, g)
                    column = counts_T[:, :, bass.ds(base, 1)].rearrange("p b a -> p (b a)")
                    nc.vector.tensor_tensor(column, column, ps_cnt[:, s, 0, 0:NB], ALU.add).then_inc(col_added, 1)

                for s in range(SL):
                    nc.vector.memset(msg[:, s, :, F + HEADS:], 1.0).then_inc(ones_ready, 1)
                targets(0, 0)
                one_hots(0, 0)
                dve.wait_ge(edges_zeroed, 1)

                def body(i, s):
                    g = SL * i + s
                    dve.wait_ge(eq_ready, g + 1)
                    dve.wait_ge(kv_arrived[s], 16 * T * (i + 1))
                    nc.vector.tensor_tensor(kq[:, :, :], kv[:, s, :, 0:F], ps_eq[:, 1, :, :], ALU.mult).then_inc(kq_done, 1)
                    dve.wait_ge(kq_done, g + 1)
                    nc.vector.tensor_tensor(kqe[:, :, :], kq[:, :, :], ps_eq[:, 0, :, :], ALU.mult).then_inc(eq_used, 1)
                    dve.wait_ge(eq_used, g + 1)
                    nc.vector.reduce_sum(score[:, :], kqe[:, :, :].rearrange("p j (h d) -> p (j h) d", d=HD), axis=X).then_inc(heads_done, 1)
                    dve.wait_ge(heads_done, g + 1)
                    lim = 5.0 * HD ** 0.5
                    nc.vector.tensor_scalar(score_c[:, :, :].rearrange("p j h -> p (j h)"), score[:, :], lim, -lim,
                                            ALU.min, ALU.max).then_inc(clip_ready, 1)
                    if exists(i, s, -1):
                        add_sums(*at(i, s, -1))
                    if exists(i, s, 1):
                        targets(*at(i, s, 1))
                        one_hots(*at(i, s, 1))
                    dve.wait_ge(exp_ready, g + 1)
                    nc.vector.tensor_tensor(
                        msg[:, s, :, 0:F].rearrange("p j (h d) -> p j h d", d=HD),
                        kv[:, s, :, F:].rearrange("p j (h d) -> p j h d", d=HD),
                        msg[:, s, :, F:F + HEADS].rearrange("p j (h a) -> p j h a", a=1).to_broadcast([P, T, HEADS, HD]),
                        ALU.mult).then_inc(msg_ready, 1)
                steps(dve, body)
                add_sums(ITER - 1, SL - 1)

            @block.tensor
            def _(pe):
                def transposes(i, s):
                    g = SL * i + s
                    pe.wait_ge(d_ready, g + 1)
                    if exists(i, s, -1):
                        pe.wait_ge(t_copied, g)
                    if isinstance(i, int) and g == NG - 1:
                        pe.wait_ge(ea_arrived[s], 16 * (i + 2))
                    else:
                        pe.wait_ge(ea_arrived[s], 16 * (i + 1))
                    for c in range(T // 2):
                        nc.tensor.transpose(ps_eT[:, c * P:(c + 1) * P],
                                            ea[:, s, 2 * c:2 * c + 2, :].rearrange("p j f -> p (j f)"), ident[:, :])
                    for j in range(T):
                        last = nc.tensor.transpose(ps_dT[0:W, j * P:(j + 1) * P], d_hot[:, s, j, :], ident[:, :])
                    last.then_inc(transposed, 1)

                def count(i, s):
                    g = SL * i + s
                    if exists(i, s, -SL):
                        pe.wait_ge(cnt_copied, g - 1)
                        pe.wait_ge(col_added, g - 1)
                    for j in range(T):
                        pe.wait_ge(hot_ready, T * g + j + 1)
                        for h in range(2):
                            last = nc.tensor.matmul(ps_cnt[:, s, h, 0:WH * NB], l_hot[:, j, :],
                                                    k_hot[:, j, h * WH * NB:(h + 1) * WH * NB],
                                                    start=(j == 0), stop=(j == T - 1))
                        last.then_inc(cnt_done, 1)

                def project(i, s):
                    g = SL * i + s
                    pe.wait_ge(t_copied, g + 1)
                    pe.wait_ge(q_arrived[s], 16 * (i + 1))
                    if exists(i, s, -1):
                        pe.wait_ge(eq_used, g)
                    for c in range(T // 2):
                        nc.tensor.matmul(ps_eq[:, 0, 2 * c:2 * c + 2, :].rearrange("p j f -> p (j f)"), ea_T[:, c, :], we_diag[:, :],
                                         start=True, stop=True)
                    for j in range(T):
                        last = nc.tensor.matmul(ps_eq[:, 1, j, :], d_hot_T[:, j, :], q_win[:, s, :], start=True, stop=True)
                    last.then_inc(eq_ready, 1)

                transposes(0, 0)
                count(0, 0)
                project(0, 0)
                pe.wait_ge(ones_ready, SL)

                def body(i, s):
                    g = SL * i + s
                    if exists(i, s, 1):
                        transposes(*at(i, s, 1))
                        count(*at(i, s, 1))
                    pe.wait_ge(msg_ready, g + 1)
                    if exists(i, s, -1):
                        pe.wait_ge(sum_added, g)
                    for j in range(T):
                        last = nc.tensor.matmul(ps_sum[0:MSG, 0:W], msg[:, s, j, :], d_hot[:, s, j, :],
                                                start=(j == 0), stop=(j == T - 1))
                    last.then_inc(sum_done, 1)
                    if exists(i, s, 1):
                        project(*at(i, s, 1))
                steps(pe, body)
        e_ctx.close()
        edge_ctx.close()

        n_ctx = ExitStack()
        y = sb(n_ctx, "y", [NP, NB, F])
        x1 = sb(n_ctx, "x1", [NP, NB, F])
        root = sb(n_ctx, "root", [NP, NB, F])
        part = sb(n_ctx, "part", [NP, 2, BB, F])
        h1 = x_sb
        sq = root
        split = sb(n_ctx, "split", [NP, NB, 3, F], bf16)
        h_T = sums_T[0:F, 0:N]
        rz = sb(n_ctx, "rz", [NP, NB, HEADS])
        rcnt = sb(n_ctx, "rcnt", [NP, NB])
        mean = sb(n_ctx, "mean", [NP, NB])
        var = sb(n_ctx, "var", [NP, NB])
        std = sb(n_ctx, "std", [NP, NB])
        eps = sb(n_ctx, "eps", [NP, 1])

        ps_a = pb(n_ctx, "ps_a", [P, 4, 512])
        ps_t = pb(n_ctx, "ps_t", [P, 2, 512])
        ps_g = pb(n_ctx, "ps_g", [P, 2, 512])
        SB = 512 // MSG
        SR = -(-NB // SB)
        PR = -(-NB // 2)
        parts_done = [sem("parts_done0"), sem("parts_done1")]

        sums_transposed = sem("sums_transposed")
        chain = sem("node_chain")
        eps_ready = sem("eps_ready")
        var_ready, std_ready = sem("var_ready"), sem("std_ready")
        h_ready = sem("h_ready")
        hT_done, hT_copied = sem("hT_done"), sem("hT_copied")
        g_done = sem("g_done")
        hi_ready = sem("hi_ready")
        rest_ready = sem("rest_ready")
        mid_ready = sem("mid_ready")
        lo_ready = sem("lo_ready")
        agg_done = sem("agg_done")
        agg_used = sem("agg_used")
        y_ready = sem("y_ready")
        stored = sem("stored")

        with nc.Block() as block:
            @block.sync
            def _(sp):
                sp.wait_ge(y_ready, 1)
                sp.dma_start(out.rearrange("(b p) f -> p b f", p=NP), y[:, :, :]).then_inc(stored, 16)
                sp.wait_ge(stored, 16)

            @block.tensor
            def _(pe):
                for b in range(NB):
                    t = nc.tensor.transpose(ps_a[0:NP, b // SB, b % SB * MSG:(b % SB + 1) * MSG],
                                            sums_T[:, b * NP:(b + 1) * NP], ident[0:MSG, 0:MSG])
                    if b % SB == SB - 1 or b == NB - 1:
                        t.then_inc(sums_transposed, 1)
                for c in range(2):
                    h = (x1, h1)[c]
                    pe.wait_ge(h_ready, c + 1)

                    def products(r):
                        n = XG * c + r
                        pe.wait_ge(hT_copied, n + 1)
                        if n >= 2:
                            pe.wait_ge(lo_ready, n - 1)
                        for b in range(BB * r, min(BB * r + BB, NB)):
                            k = b - BB * r
                            last = nc.tensor.matmul(ps_g[0:NP, n % 2, k * 2 * F:(k + 1) * 2 * F],
                                                    h_T[:, b * NP:(b + 1) * NP], wl_wr_T[:, c, :], start=True, stop=True)
                        last.then_inc(g_done, 1)

                    for r in range(XG):
                        n = XG * c + r
                        if n >= 2:
                            pe.wait_ge(hT_copied, n - 1)
                        for b in range(BB * r, min(BB * r + BB, NB)):
                            k = b - BB * r
                            last = nc.tensor.transpose(ps_t[0:F, n % 2, k * NP:(k + 1) * NP], h[:, b, :], ident[0:NP, 0:NP])
                        last.then_inc(hT_done, 1)
                        if r:
                            products(r - 1)
                    products(XG - 1)
                    for q in range(PR):
                        n = PR * c + q
                        if n >= 4:
                            pe.wait_ge(agg_used, n - 3)
                        for b in range(2 * q, min(2 * q + 2, NB)):
                            for a in range(NB):
                                if q == 0 and b == 0 and a % BB == 0:
                                    pe.wait_ge(lo_ready, XG * c + a // BB + 1)
                                    pe.wait_ge(mid_ready, XG * c + a // BB + 1)
                                last = nc.tensor.matmul(ps_a[:, n % 4, b % 2 * 3 * F:(b % 2 + 1) * 3 * F],
                                                        counts_T[0:NP, a, b * NP:b * NP + P],
                                                        split[:, a, :, :].rearrange("p c f -> p (c f)"),
                                                        start=(a == 0), stop=(a == NB - 1))
                        last.then_inc(agg_done, 1)

            @block.scalar
            def _(act):
                def root_of_variance(c):
                    act.wait_ge(var_ready, c + 1)
                    nc.scalar.activation(std[:, :], var[:, :], ACT.Sqrt, bias=eps[:, 0:1], scale=1.0 / F).then_inc(std_ready, 1)

                act.wait_ge(eps_ready, 1)
                root_of_variance(0)
                for c in range(2):
                    def first_parts(r):
                        n = XG * c + r
                        b0, k = BB * r, min(BB, NB - BB * r)
                        act.wait_ge(g_done, n + 1)
                        if c and r == 0:
                            act.wait_ge(agg_done, PR)
                        nc.scalar.activation(split[:, b0:b0 + k, 0, :],
                                             ps_g[0:NP, n % 2, 0:k * 2 * F].rearrange("p (k f) -> p k f", f=2 * F)[:, :, 0:F],
                                             ACT.Copy).then_inc(hi_ready, 1)

                    def second_parts(r):
                        n = XG * c + r
                        b0, k = BB * r, min(BB, NB - BB * r)
                        act.wait_ge(rest_ready, n + 1)
                        nc.scalar.activation(split[:, b0:b0 + k, 1, :], part[:, n % 2, 0:k, :], ACT.Copy).then_inc(mid_ready, 1)

                    for r in range(XG + 2):
                        if r < XG:
                            n = XG * c + r
                            w = min(BB, NB - BB * r) * NP
                            act.wait_ge(hT_done, n + 1)
                            nc.scalar.activation(h_T[:, BB * r * NP:BB * r * NP + w], ps_t[0:F, n % 2, 0:w], ACT.Copy).then_inc(hT_copied, 1)
                        if r and r <= XG:
                            first_parts(r - 1)
                        if r >= 2:
                            second_parts(r - 2)
                root_of_variance(1)

            @block.vector
            def _(dve):
                steps_done = [0]

                def after(ins):
                    steps_done[0] += 1
                    ins.then_inc(chain, 1)
                    dve.wait_ge(chain, steps_done[0])

                def wide(a, k=F):
                    return a.rearrange("p (b a) -> p b a", a=1).to_broadcast([NP, NB, k])

                def norm(c, to):
                    after(nc.vector.reduce_sum(mean[:, :], y[:, :, :], axis=X))
                    after(nc.vector.tensor_scalar(mean[:, :], mean[:, :], 1.0 / F, None, ALU.mult))
                    after(nc.vector.tensor_tensor(y[:, :, :], y[:, :, :], wide(mean[:, :]), ALU.subtract))
                    after(nc.vector.tensor_tensor(sq[:, :, :], y[:, :, :], y[:, :, :], ALU.mult))
                    nc.vector.reduce_sum(var[:, :], sq[:, :, :], axis=X).then_inc(var_ready, 1)
                    dve.wait_ge(std_ready, c + 1)
                    after(nc.vector.reciprocal(std[:, :], std[:, :]))
                    return nc.vector.tensor_tensor(to, y[:, :, :], wide(std[:, :]), ALU.mult)

                nc.vector.memset(eps[:, :], EPS).then_inc(eps_ready, 1)
                for q in range(SR):
                    b0, k = SB * q, min(SB, NB - SB * q)
                    dve.wait_ge(sums_transposed, q + 1)
                    sums = ps_a[0:NP, q, 0:k * MSG].rearrange("p (b m) -> p b m", m=MSG)
                    nc.vector.tensor_scalar(rcnt[:, b0:b0 + k], sums[:, :, F + HEADS], 1.0, None, ALU.max)
                    after(nc.vector.tensor_scalar(rz[:, b0:b0 + k, :], sums[:, :, F:F + HEADS], 1e-6, None, ALU.add))
                    after(nc.vector.reciprocal(rz[:, b0:b0 + k, :], rz[:, b0:b0 + k, :]))
                    for h in range(HEADS):
                        last = nc.vector.tensor_tensor(
                            y[:, b0:b0 + k, h * HD:(h + 1) * HD], sums[:, :, h * HD:(h + 1) * HD],
                            rz[:, b0:b0 + k, h:h + 1].to_broadcast([NP, k, HD]), ALU.mult)
                    after(last)
                after(nc.vector.tensor_tensor(y[:, :, :], y[:, :, :], x_sb[:, :, :], ALU.add))
                nc.vector.reciprocal(rcnt[:, :], rcnt[:, :])
                norm(0, x1[:, :, :]).then_inc(h_ready, 1)

                for c in range(2):
                    to = (h1, y)[c]
                    for r in range(XG):
                        n = XG * c + r
                        b0, k = BB * r, min(BB, NB - BB * r)
                        prod = ps_g[0:NP, n % 2, 0:k * 2 * F].rearrange("p (k f) -> p k f", f=2 * F)
                        dve.wait_ge(hi_ready, n + 1)
                        if n >= 2:
                            dve.wait_ge(mid_ready, n - 1)
                        nc.vector.tensor_tensor(part[:, n % 2, 0:k, :], prod[:, :, 0:F], split[:, b0:b0 + k, 0, :],
                                                ALU.subtract).then_inc(rest_ready, 1)
                        nc.vector.tensor_tensor(root[:, b0:b0 + k, :], prod[:, :, F:],
                                                bias[0:NP, c:c + 1, :].to_broadcast([NP, k, F]), ALU.add)
                        dve.wait_ge(mid_ready, n + 1)
                        nc.vector.tensor_tensor(split[:, b0:b0 + k, 2, :], part[:, n % 2, 0:k, :], split[:, b0:b0 + k, 1, :],
                                                ALU.subtract).then_inc(lo_ready, 1)
                    for q in range(PR):
                        n = PR * c + q
                        b0, k = 2 * q, min(2, NB - 2 * q)
                        dve.wait_ge(agg_done, n + 1)
                        last = nc.vector.reduce_sum(to[:, b0:b0 + k, :],
                                                    ps_a[0:NP, n % 4, 0:k * 3 * F].rearrange("p (b c f) -> p b f c", c=3, f=F), axis=X)
                        last.then_inc(agg_used, 1)
                        dve.wait_ge(agg_used, n + 1)
                        for b in range(b0, b0 + k):
                            last = nc.vector.scalar_tensor_tensor(out=to[:, b, :], in0=to[:, b, :], scalar=rcnt[:, b:b + 1],
                                                                  in1=root[:, b, :], op0=ALU.mult, op1=ALU.add)
                        after(last)
                        last = nc.vector.tensor_scalar(to[:, b0:b0 + k, :], to[:, b0:b0 + k, :], 0.0, None, ALU.max)
                        after(last)
                    if c == 0:
                        nc.vector.nop().then_inc(h_ready, 1)
                after(nc.vector.tensor_tensor(y[:, :, :], y[:, :, :], x1[:, :, :], ALU.add))
                norm(1, y[:, :, :]).then_inc(y_ready, 1)
        n_ctx.close()
        counts_ctx.close()

_INS = ["x", "src", "dst", "edge_attr_64", "L0_gnn_Wq", "L0_gnn_Wk", "L0_gnn_We", "L0_gnn_Wv", "L1_gnn_W_l1",
        "L1_gnn_b1", "L1_gnn_W_r1", "L1_gnn_W_l2", "L1_gnn_b2", "L1_gnn_W_r2"]


def kernel(**inputs):
    import numpy as np
    import concourse.bacc as bacc
    from concourse import mybir
    from concourse.bass_utils import run_bass_kernel_spmd as run

    nc = bacc.Bacc("TRN2", target_bir_lowering=False, num_devices=1)
    arrays, args = {}, []
    for name in _INS:
        a = np.ascontiguousarray(inputs[name])
        arrays[f"in_{name}"] = a
        args.append(nc.dram_tensor(f"in_{name}", a.shape, mybir.dt.from_np(a.dtype), kind="ExternalInput").ap())
    n, f = inputs["x"].shape
    args.append(nc.dram_tensor("out_0", (n, f), mybir.dt.float32, kind="ExternalOutput").ap())
    gnn_kernel(nc, *args)
    return run(nc, [arrays], core_ids=[0]).results[0]["out_0"]
```

```python
import concourse.bass as bass
from concourse import mybir
from contextlib import ExitStack


def gnn_kernel(nc, x, src, dst, edge_attr, Wq, Wk, We, Wv, Wl1, b1, Wr1, Wl2, b2, Wr2, out):
    f32, bf16, f16, i32 = mybir.dt.float32, mybir.dt.bfloat16, mybir.dt.float16, mybir.dt.int32
    ALU = mybir.AluOpType
    ACT = mybir.ActivationFunctionType
    X = mybir.AxisListType.X

    N, F = x.shape
    E = src.shape[0]
    HEADS = 4
    HD = F // HEADS
    P = 128
    NB = 25
    NP = N // NB
    T = 4
    GE = P * T
    NG = -(-E // GE)
    TAIL = E - (NG - 1) * GE
    TFULL, TREST = TAIL // T, TAIL % T
    W = 40
    WH = W // 2
    KEYS = W * NB
    NW = N + W
    MSG = F + HEADS + 1
    FAR = 1 << 20
    DUP = 127
    MAGIC = 1.5 * 2.0 ** 23
    EPS = 1e-5
    BB = 4

    ctx = ExitStack()
    with ctx:
        def sb(stack, name, shape, dt=f32, side="left"):
            return stack.enter_context(nc.sbuf_tensor(name, shape, dt, side=side))

        def pb(stack, name, shape):
            return stack.enter_context(nc.psum_tensor(name, shape, f32))

        def sem(name):
            return ctx.enter_context(nc.semaphore(name))

        kv_table = nc.dram_tensor("kv_table", (N, 2 * F), f32, kind="Internal").ap()
        q_table = nc.dram_tensor("q_table", (NW, F), f32, kind="Internal").ap()

        ident = sb(ctx, "ident", [P, P])
        wl_wr_T = sb(ctx, "wl_wr_T", [F, 2, 2 * F])
        bias = sb(ctx, "bias", [P, 2, F])
        sums_T = sb(ctx, "sums_T", [MSG, NW])

        s_load, s_wload, s_xload, s_idx = sem("rows_loaded"), sem("weights_loaded"), sem("x_loaded"), sem("bias_loaded")
        s_pad = sem("padding_written")
        s_id = sem("identity_ready")
        s_rowsf = sem("rows_converted")
        s_checked = sem("rows_checked")
        s_odd = sem("irregularities_summed")
        s_idT = sem("index_transposed")
        s_base = sem("base_row_ready")
        s_bb = sem("base_broadcast")
        s_tab = sem("table_chain")
        s_tabs = sem("tables_ready")
        s_iota = sem("iota_ready")
        s_wT, s_wc = sem("weights_transposed"), sem("weights_copied")
        s_xT, s_xc = sem("x_transposed"), sem("x_copied")
        s_proj, s_projc = sem("projected"), sem("projection_copied")
        s_tstore = sem("tables_stored")
        s_zero = sem("zeros_ready")

        edge_ctx = ExitStack()
        src_i = sb(edge_ctx, "src_i", [P, NG, T], i32)
        lo_tab = sb(edge_ctx, "lo_tab", [P, NG, T])
        one = sb(edge_ctx, "one", [P, 1])
        key_tab = sb(edge_ctx, "key_tab", [P, NG, T], f16)
        rel_tab = sb(edge_ctx, "rel_tab", [P, NG, T])
        odd = sb(edge_ctx, "odd", [1, 1], i32)
        base_now = sb(edge_ctx, "base_now", [1, NG], i32)
        base_last = sb(edge_ctx, "base_last", [1, NG + 1], i32)
        iota = sb(edge_ctx, "iota", [P, KEYS], f16)
        we_diag = sb(edge_ctx, "we_diag", [P, P])

        tab_ctx = ExitStack()
        rows_i = sb(tab_ctx, "rows_i", [NG, 2, GE], i32, side="right")
        next_i = sb(tab_ctx, "next_i", [NG, GE], i32, side="right")
        next_f = sb(tab_ctx, "next_f", [NG, GE], side="right")
        late = sb(tab_ctx, "late", [NG, 2, GE], side="right")
        irregular = sb(tab_ctx, "irregular", [NG, 2], side="right")
        ones_col = sb(tab_ctx, "ones_col", [P, 1], side="right")
        rows_f = sb(tab_ctx, "rows_f", [NG, 2, GE], side="right")
        src_f = sb(tab_ctx, "src_f", [P, NG, T], side="right")
        dst_f = sb(tab_ctx, "dst_f", [P, NG, T], side="right")
        hi_tab = sb(tab_ctx, "hi_tab", [P, NG, T], side="right")
        in_tab = sb(tab_ctx, "in_tab", [P, NG, T], side="right")
        iota_i = sb(tab_ctx, "iota_i", [P, KEYS], i32, side="right")
        ones_row = sb(tab_ctx, "ones_row", [1, P], side="right")
        x_sb = sb(tab_ctx, "x_sb", [NP, NB, F], side="right")
        w_kv = sb(tab_ctx, "w_kv", [2 * F, F], side="right")
        w_q = sb(tab_ctx, "w_q", [F, F], side="right")
        w_ee = sb(tab_ctx, "w_ee", [F, 2, F], side="right")
        w_s = sb(tab_ctx, "w_s", [2 * F, 2, F], side="right")
        w_kvq_T = sb(tab_ctx, "w_kvq_T", [F, 3 * F], side="right")
        x_T = sb(tab_ctx, "x_T", [F, N], side="right")
        kvq = sb(tab_ctx, "kvq", [NP, NB, 3 * F], side="right")
        zeros = sb(tab_ctx, "zeros", [W, F], side="right")

        ps_s = pb(tab_ctx, "ps_s", [P, 512])
        ps_d = pb(tab_ctx, "ps_d", [P, 512])
        ps_b = pb(tab_ctx, "ps_b", [P, 512])
        ps_w = pb(tab_ctx, "ps_w", [P, 512])
        ps_x = pb(tab_ctx, "ps_x", [P, 2, 512])
        ps_k = pb(tab_ctx, "ps_k", [P, 2, 512])
        XG = -(-NB // BB)

        with nc.Block() as block:
            @block.sync
            def _(sp):
                sp.dma_start(w_kv[0:F, :], Wk).then_inc(s_wload, 16)
                sp.dma_start(w_kv[F:, :], Wv).then_inc(s_wload, 16)
                sp.dma_start(w_q[:, :], Wq).then_inc(s_wload, 16)
                sp.dma_start(x_sb[:, :, :], x.rearrange("(b p) f -> p b f", p=NP)).then_inc(s_xload, 16)
                sp.dma_start(w_ee[:, :, :], We.rearrange("o (a f) -> o a f", a=1).to_broadcast([F, 2, F])).then_inc(s_wload, 16)
                for c, (wl, wr) in enumerate([(Wl1, Wr1), (Wl2, Wr2)]):
                    sp.dma_start(w_s[0:F, c, :], wl).then_inc(s_wload, 16)
                    sp.dma_start(w_s[F:, c, :], wr).then_inc(s_wload, 16)
                for c, b in enumerate((b1, b2)):
                    sp.dma_start(bias[:, c, :], b.rearrange("(a f) -> a f", a=1).to_broadcast([P, F])).then_inc(s_idx, 16)
                sp.wait_ge(s_zero, 1)
                sp.dma_start(q_table[N:NW, :], zeros[:, :]).then_inc(s_tstore, 16)
                for r in range(0, NB, 8):
                    k = min(8, NB - r)
                    sp.wait_ge(s_projc, min(r + 8, NB))
                    sp.dma_start(kv_table.rearrange("(b p) f -> p b f", p=NP)[:, r:r + k, :],
                                 kvq[:, r:r + k, 0:2 * F]).then_inc(s_tstore, 16)
                    sp.dma_start(q_table[0:N, :].rearrange("(b p) f -> p b f", p=NP)[:, r:r + k, :],
                                 kvq[:, r:r + k, 2 * F:]).then_inc(s_tstore, 16)
                sp.wait_ge(s_idx, 32)
                sp.wait_ge(s_tstore, 16 * (1 + 2 * (-(-NB // 8))))

            @block.scalar
            def _(act):
                def keep_projections(r):
                    for b in range(BB * r, min(BB * r + BB, NB), 2):
                        k = min(2, NB - b)
                        act.wait_ge(s_proj, b + k)
                        nc.scalar.activation(kvq[:, b:b + k, :].rearrange("p b f -> p (b f)"),
                                             ps_k[0:NP, b // 2 % 2, 0:k * 3 * F], ACT.Copy).then_inc(s_projc, k)

                for r in range(XG):
                    n = min(BB, NB - BB * r) * NP
                    act.wait_ge(s_xT, r + 1)
                    nc.scalar.activation(x_T[:, BB * r * NP:BB * r * NP + n], ps_x[0:F, r % 2, 0:n],
                                         ACT.Copy).then_inc(s_xc, 1)
                    if r:
                        keep_projections(r - 1)
                keep_projections(XG - 1)

            @block.gpsimd
            def _(pool):
                nc.gpsimd.memset(rows_i[:, 0, :], 0).then_inc(s_pad, 1)
                nc.gpsimd.memset(rows_i[:, 1, :], FAR).then_inc(s_pad, 1)
                nc.gpsimd.memset(next_i[:, :], N - 1).then_inc(s_pad, 1)
                pool.wait_ge(s_pad, 3)
                for c, a in enumerate((src, dst)):
                    pool.dma_start(rows_i[0:NG - 1, c, :],
                                  a[0:(NG - 1) * GE].rearrange("(g e) -> g e", e=GE)).then_inc(s_load, 16)
                    pool.dma_start(rows_i[NG - 1:NG, c, 0:TAIL],
                                  a[(NG - 1) * GE:E].rearrange("(g e) -> g e", g=1)).then_inc(s_load, 16)
                pool.dma_start(next_i[0:NG - 1, :],
                              dst[1:(NG - 1) * GE + 1].rearrange("(g e) -> g e", e=GE)).then_inc(s_load, 16)
                pool.dma_start(next_i[NG - 1:NG, 0:TAIL - 1],
                              dst[(NG - 1) * GE + 1:E].rearrange("(g e) -> g e", g=1)).then_inc(s_load, 16)
                nc.gpsimd.memset(zeros[:, :], 0.0).then_inc(s_zero, 1)
                nc.gpsimd.memset(ident[:, :], 0.0).then_inc(s_id, 1)
                nc.gpsimd.memset(ones_row[:, :], 1.0).then_inc(s_id, 1)
                nc.gpsimd.memset(ones_col[:, :], 1.0).then_inc(s_id, 1)
                pool.wait_ge(s_id, 3)
                nc.gpsimd.affine_select(out=ident[:, :], in_=ident[:, :], compare_op=ALU.not_equal, fill=1.0,
                                        base=0, pattern=[[-1, P]], channel_multiplier=1).then_inc(s_id, 1)
                nc.gpsimd.iota(iota_i[:, :], [[1, KEYS]], base=0, channel_multiplier=0).then_inc(s_iota, 1)
                nc.gpsimd.memset(sums_T[:, :], 0.0).then_inc(s_zero, 1)
                nc.gpsimd.memset(we_diag[:, :], 0.0).then_inc(s_zero, 1)

            @block.tensor
            def _(pe):
                pe.wait_ge(s_id, 4)
                pe.wait_ge(s_wload, 16 * 8)
                nc.tensor.transpose(ps_w[0:F, 0:P], w_kv[:, :], ident[:, :])
                nc.tensor.transpose(ps_w[0:F, P:P + F], w_q[:, :], ident[0:F, 0:F])
                nc.tensor.transpose(ps_w[:, P + F:2 * P], w_ee[:, :, :].rearrange("p a f -> p (a f)"), ident[0:F, 0:F])
                nc.tensor.transpose(ps_w[0:F, 2 * P:3 * P], w_s[:, 0, :], ident[:, :])
                nc.tensor.transpose(ps_w[0:F, 3 * P:4 * P], w_s[:, 1, :], ident[:, :]).then_inc(s_wT, 1)
                pe.wait_ge(s_xload, 16)

                def project(r):
                    pe.wait_ge(s_xc, r + 1)
                    for b in range(BB * r, min(BB * r + BB, NB)):
                        if b >= 4 and b % 2 == 0:
                            pe.wait_ge(s_projc, b - 2)
                        nc.tensor.matmul(ps_k[0:NP, b // 2 % 2, b % 2 * 3 * F:(b % 2 + 1) * 3 * F],
                                         x_T[:, b * NP:(b + 1) * NP], w_kvq_T[:, :],
                                         start=True, stop=True).then_inc(s_proj, 1)

                for r in range(XG):
                    if r >= 2:
                        pe.wait_ge(s_xc, r - 1)
                    for b in range(BB * r, min(BB * r + BB, NB)):
                        t = nc.tensor.transpose(ps_x[0:F, r % 2, (b - BB * r) * NP:(b - BB * r + 1) * NP],
                                                x_sb[:, b, :], ident[0:NP, 0:NP])
                    t.then_inc(s_xT, 1)
                    if r == 0:
                        pe.wait_ge(s_rowsf, 2)
                        for c, ps in enumerate((ps_s, ps_d)):
                            for j in range(T):
                                nc.tensor.transpose(ps[:, j * NG:(j + 1) * NG], rows_f[:, c, j::T],
                                                    ident[0:NG, 0:NG]).then_inc(s_idT, 1)
                        pe.wait_ge(s_wc, 2)
                        pe.wait_ge(s_base, 1)
                        nc.tensor.matmul(ps_b[:, 0:NG], ones_row[:, :], dst_f[0:1, :, 0],
                                         start=True, stop=True).then_inc(s_bb, 1)
                    else:
                        project(r - 1)
                project(XG - 1)
                pe.wait_ge(s_checked, 1)
                nc.tensor.matmul(ps_w[0:1, 0:1], irregular[:, 0:1], ones_col[0:NG, :], start=True, stop=True).then_inc(s_odd, 1)

            @block.vector
            def _(dve):
                steps = [0]

                def after(ins):
                    steps[0] += 1
                    ins.then_inc(s_tab, 1)
                    dve.wait_ge(s_tab, steps[0])

                dve.wait_ge(s_load, 96)
                for c in range(2):
                    nc.vector.tensor_copy(rows_f[:, c, :], rows_i[:, c, :]).then_inc(s_rowsf, 1)
                dve.wait_ge(s_wT, 1)
                dve.wait_ge(s_zero, 3)
                nc.vector.tensor_copy(w_kvq_T[:, :], ps_w[0:F, 0:3 * F]).then_inc(s_wc, 1)
                nc.vector.tensor_copy(wl_wr_T[:, :, :].rearrange("p a f -> p (a f)"), ps_w[0:F, 2 * P:4 * P])
                nc.vector.tensor_copy(we_diag[0:F, 0:F], ps_w[0:F, P + F:2 * P])
                nc.vector.tensor_copy(we_diag[F:, F:], ps_w[F:, P + F:2 * P]).then_inc(s_wc, 1)
                dve.wait_ge(s_idT, T)
                after(nc.vector.tensor_copy(src_f[:, :, :], ps_s[:, 0:T * NG].rearrange("p (j g) -> p g j", j=T)))
                nc.vector.tensor_copy(src_i[:, :, :], src_f[:, :, :])
                dve.wait_ge(s_idT, 2 * T)
                nc.vector.tensor_copy(dst_f[:, :, :], ps_d[:, 0:T * NG].rearrange("p (j g) -> p g j", j=T)).then_inc(s_base, 1)
                dve.wait_ge(s_base, 1)
                nc.vector.tensor_copy(base_now[:, :], dst_f[0:1, :, 0])
                nc.vector.tensor_copy(base_last[:, 0:1], dst_f[0:1, 0, 0:1])
                nc.vector.tensor_copy(base_last[:, 1:NG + 1], dst_f[0:1, :, 0])

                after(nc.vector.tensor_scalar(hi_tab[:, :, :], src_f[:, :, :], 1.0 / NP, -(NP // 2) / NP, ALU.mult, ALU.add))
                after(nc.vector.tensor_scalar(hi_tab[:, :, :], hi_tab[:, :, :], MAGIC, -MAGIC, ALU.add, ALU.add))
                nc.vector.scalar_tensor_tensor(out=lo_tab[:, :, :], in0=hi_tab[:, :, :], scalar=float(NP),
                                               in1=src_f[:, :, :], op0=ALU.mult, op1=ALU.subtract)
                nc.vector.memset(one[:, :], 1.0)
                dve.wait_ge(s_bb, 1)
                after(nc.vector.tensor_tensor(rel_tab[:, :, :], dst_f[:, :, :],
                                              ps_b[:, 0:NG].rearrange("p (g a) -> p g a", a=1).to_broadcast([P, NG, T]), ALU.subtract))
                nc.vector.scalar_tensor_tensor(out=hi_tab[:, :, :], in0=rel_tab[:, :, :], scalar=float(NB),
                                               in1=hi_tab[:, :, :], op0=ALU.mult, op1=ALU.add)
                after(nc.vector.tensor_scalar(in_tab[:, :, :], rel_tab[:, :, :], float(W), None, ALU.is_lt))
                after(nc.vector.scalar_tensor_tensor(out=hi_tab[:, :, :], in0=hi_tab[:, :, :], scalar=1.0,
                                                     in1=in_tab[:, :, :], op0=ALU.add, op1=ALU.mult))
                nc.vector.tensor_scalar(key_tab[:, :, :], hi_tab[:, :, :], -1.0, None, ALU.add)
                dve.wait_ge(s_iota, 1)
                nc.vector.tensor_copy(iota[:, :], iota_i[:, :])
                targets, first = rows_f[:, 1, :], rows_f[:, 1, 0:1]
                nc.vector.tensor_copy(next_f[:, :], next_i[:, :])
                after(nc.vector.tensor_scalar(late[:, 0, :], targets, float(N - 1), None, ALU.min))
                after(nc.vector.tensor_tensor(late[:, 0, :], next_f[:, :], late[:, 0, :], ALU.is_lt))
                after(nc.vector.tensor_scalar(late[:, 1, :], next_f[:, :], first, float(W), ALU.subtract, ALU.is_ge))
                after(nc.vector.tensor_tensor(next_f[:, 0:GE - DUP], rows_f[:, 1, DUP:], rows_f[:, 1, 0:GE - DUP], ALU.is_equal))
                nc.vector.reduce_sum(irregular[:, 0:1], late[:, :, :].rearrange("p a e -> p (a e)"), axis=X)
                after(nc.vector.reduce_sum(irregular[:, 1:2], next_f[:, 0:GE - DUP], axis=X))
                after(nc.vector.tensor_tensor(irregular[:, 0:1], irregular[:, 0:1], irregular[:, 1:2], ALU.add))
                after(nc.vector.tensor_tensor(irregular[0:1, 0:1], irregular[0:1, 0:1], rows_f[0:1, 1, 0:1], ALU.add))
                nc.vector.nop().then_inc(s_checked, 1)
                dve.wait_ge(s_odd, 1)
                nc.vector.tensor_copy(odd[:, :], ps_w[0:1, 0:1])

        def norm(dve, after, y, sq, mean, var, std, var_ready, std_ready, n, to):
            def wide(a):
                return a.rearrange("p (b a) -> p b a", a=1).to_broadcast([NP, NB, F])

            after(nc.vector.reduce_sum(mean[:, :], y[:, :, :], axis=X))
            after(nc.vector.tensor_scalar(mean[:, :], mean[:, :], 1.0 / F, None, ALU.mult))
            after(nc.vector.tensor_tensor(y[:, :, :], y[:, :, :], wide(mean[:, :]), ALU.subtract))
            after(nc.vector.tensor_tensor(sq[:, :, :], y[:, :, :], y[:, :, :], ALU.mult))
            nc.vector.reduce_sum(var[:, :], sq[:, :, :], axis=X).then_inc(var_ready, 1)
            dve.wait_ge(std_ready, n)
            after(nc.vector.reciprocal(std[:, :], std[:, :]))
            return nc.vector.tensor_tensor(to, y[:, :, :], wide(std[:, :]), ALU.mult)

        is_odd = nc.values_load(odd[0:1, 0:1], min_val=0, max_val=1 << 24,
                                skip_runtime_bounds_check_because="only compared with 0")
        with nc.If(is_odd > 0):
            g_ctx = ExitStack()
            WINS = 7
            WIDE = -(-N // WINS)
            h_table = nc.dram_tensor("h_table", (N, F), f32, kind="Internal").ap()
            src_one = sb(g_ctx, "src_one", [P, T], i32)
            dst_one = sb(g_ctx, "dst_one", [P, T], i32)
            rows = sb(g_ctx, "rows", [P, T, 2 * F])
            q_rows = sb(g_ctx, "q_rows", [P, T, F])
            ea_one = sb(g_ctx, "ea_one", [P, T, F])
            ea_one_T = sb(g_ctx, "ea_one_T", [P, T // 2, P])
            part_s = sb(g_ctx, "part_s", [P, T, F])
            score_s = sb(g_ctx, "score_s", [P, T * HEADS])
            msg_s = sb(g_ctx, "msg_s", [P, T, MSG])
            wide_hot = sb(g_ctx, "wide_hot", [P, T, WIDE])
            y_s = sb(g_ctx, "y_s", [NP, NB, F])
            x1_s = sb(g_ctx, "x1_s", [NP, NB, F])
            h1_s = sb(g_ctx, "h1_s", [NP, NB, F])
            sq_s = sb(g_ctx, "sq_s", [NP, NB, F])
            hT_s = sb(g_ctx, "hT_s", [F, NP])
            rz_s = sb(g_ctx, "rz_s", [NP, NB, HEADS])
            rcnt_s = sb(g_ctx, "rcnt_s", [NP, NB])
            mean_s = sb(g_ctx, "mean_s", [NP, NB])
            var_s = sb(g_ctx, "var_s", [NP, NB])
            std_s = sb(g_ctx, "std_s", [NP, NB])
            eps_s = sb(g_ctx, "eps_s", [NP, 1])
            ps_t_s, ps_e_s, ps_m_s = ps_s, ps_d, ps_b

            def groups(eng, body):
                body(0)
                with eng.Fori(1, NG - 1) as g:
                    body(g)
                body(NG - 1)

            def segment_sums(c):
                idx_set, rows_in = sem(f"idx_set{c}"), sem(f"rows_in{c}")
                go, ea_in, ea_T_done = sem(f"go{c}"), sem(f"ea_in{c}"), sem(f"ea_T_done{c}")
                ea_T_kept, e_done = sem(f"ea_T_kept{c}"), sem(f"e_done{c}")
                own, scored, weighted = sem(f"own{c}"), sem(f"scored{c}"), sem(f"weighted{c}")
                hot_set, win_done, win_added = sem(f"hot_set{c}"), sem(f"win_done{c}"), sem(f"win_added{c}")
                width = MSG if c == 0 else F
                arrivals = 16 * T * (2 if c == 0 else 1)
                with nc.Block() as block:
                    @block.sync
                    def _(sp):
                        def body(g):
                            if not isinstance(g, int) or g:
                                sp.wait_ge(ea_T_done, g)
                            if isinstance(g, int) and g == NG - 1:
                                sp.dma_start(ea_one[0:TFULL, :, :],
                                             edge_attr[g * GE:g * GE + TFULL * T, :].rearrange("(p j) f -> p j f", j=T)).then_inc(ea_in, 16)
                                sp.dma_start(ea_one[TFULL:TFULL + 1, 0:TREST, :],
                                             edge_attr[g * GE + TFULL * T:E, :].rearrange("(p j) f -> p j f", p=1)).then_inc(ea_in, 16)
                            else:
                                sp.dma_start(ea_one[:, :, :],
                                             edge_attr[bass.ds(g * GE, GE), :].rearrange("(p j) f -> p j f", j=T)).then_inc(ea_in, 16)
                        if c == 0:
                            groups(sp, body)

                    @block.gpsimd
                    def _(pool):
                        def body(g):
                            pool.wait_ge(idx_set, g + 1)
                            pool.sem_inc(go, 1)
                            for j in range(T):
                                table, to = (kv_table, rows[:, j, :]) if c == 0 else (h_table, msg_s[:, j, 0:F])
                                nc.gpsimd.indirect_dma_start(to, None, table[:, :],
                                                             bass.IndirectOffsetOnAxis(ap=src_one[:, j:j + 1], axis=0)
                                                             ).then_inc(rows_in, 16)
                                if c == 0:
                                    nc.gpsimd.indirect_dma_start(q_rows[:, j, :], None, q_table[:, :],
                                                                 bass.IndirectOffsetOnAxis(ap=dst_one[:, j:j + 1], axis=0)
                                                                 ).then_inc(rows_in, 16)
                        groups(pool, body)

                    @block.scalar
                    def _(act):
                        def body(g):
                            act.wait_ge(ea_T_done, g + 1)
                            if not isinstance(g, int) or g:
                                act.wait_ge(e_done, g)
                            nc.scalar.activation(ea_one_T[:, :, :].rearrange("p j e -> p (j e)"), ps_t_s[:, 0:T // 2 * P],
                                                 ACT.Copy).then_inc(ea_T_kept, 1)
                            act.wait_ge(scored, g + 1)
                            nc.scalar.activation(msg_s[:, :, F:F + HEADS], score_s[:, :].rearrange("p (j h) -> p j h", h=HEADS),
                                                 ACT.Exp, scale=1.0 / HD ** 0.5).then_inc(weighted, 1)
                        if c == 0:
                            groups(act, body)

                    @block.vector
                    def _(dve):
                        OWN = 3 if c == 0 else 0

                        def body(g):
                            first = isinstance(g, int) and g == 0
                            nc.vector.tensor_copy(src_one[:, :], src_i[:, bass.ds(g, 1), :].rearrange("p a j -> p (a j)"))
                            nc.vector.tensor_scalar(dst_one[:, :], dst_f[:, bass.ds(g, 1), :].rearrange("p a j -> p (a j)"),
                                                    float(N - 1), None, ALU.min).then_inc(idx_set, 1)
                            dve.wait_ge(rows_in, arrivals * (g + 1) if isinstance(g, int) else g * arrivals + arrivals)
                            if c == 0:
                                nc.vector.tensor_tensor(part_s[:, :, :], rows[:, :, 0:F], q_rows[:, :, :], ALU.mult).then_inc(own, 1)
                                dve.wait_ge(own, OWN * g + 1)
                                dve.wait_ge(e_done, g + 1)
                                nc.vector.tensor_tensor(part_s[:, :, :], part_s[:, :, :],
                                                        ps_e_s[:, 0:T * F].rearrange("p (j f) -> p j f", f=F), ALU.mult).then_inc(own, 1)
                                dve.wait_ge(own, OWN * g + 2)
                                nc.vector.reduce_sum(score_s[:, :], part_s[:, :, :].rearrange("p j (h d) -> p (j h) d", d=HD), axis=X).then_inc(own, 1)
                                dve.wait_ge(own, OWN * g + 3)
                                lim = 5.0 * HD ** 0.5
                                nc.vector.tensor_scalar(score_s[:, :], score_s[:, :], lim, -lim, ALU.min, ALU.max).then_inc(scored, 1)
                                dve.wait_ge(weighted, g + 1)
                                nc.vector.tensor_tensor(
                                    msg_s[:, :, 0:F].rearrange("p j (h d) -> p j h d", d=HD),
                                    rows[:, :, F:].rearrange("p j (h d) -> p j h d", d=HD),
                                    msg_s[:, :, F:F + HEADS].rearrange("p j (h a) -> p j h a", a=1).to_broadcast([P, T, HEADS, HD]),
                                    ALU.mult)
                            for w in range(WINS):
                                for j in range(T):
                                    last = nc.vector.tensor_scalar(wide_hot[:, j, :], iota[:, 0:WIDE], float(w * WIDE),
                                                                   dst_f[:, bass.ds(g, 1), j:j + 1].rearrange("p a j -> p (a j)"),
                                                                   ALU.add, ALU.is_equal)
                                last.then_inc(hot_set, 1)
                                dve.wait_ge(win_done, WINS * g + w + 1)
                                if not first:
                                    dve.wait_ge(win_added, WINS * g - WINS + w + 1)
                                window = sums_T[0:width, w * WIDE:(w + 1) * WIDE]
                                nc.vector.tensor_tensor(window, window, ps_m_s[0:width, 0:WIDE], ALU.add).then_inc(win_added, 1)

                        if c == 0:
                            nc.vector.memset(msg_s[:, :, F + HEADS:], 1.0)
                        groups(dve, body)

                    @block.tensor
                    def _(pe):
                        def body(g):
                            if c == 0:
                                if isinstance(g, int) and g == NG - 1:
                                    pe.wait_ge(ea_in, 16 * (g + 2))
                                else:
                                    pe.wait_ge(ea_in, 16 * g + 16)
                                for k in range(T // 2):
                                    last = nc.tensor.transpose(ps_t_s[:, k * P:(k + 1) * P],
                                                               ea_one[:, 2 * k:2 * k + 2, :].rearrange("p j f -> p (j f)"), ident[:, :])
                                last.then_inc(ea_T_done, 1)
                                pe.wait_ge(ea_T_kept, g + 1)
                                for k in range(T // 2):
                                    last = nc.tensor.matmul(ps_e_s[:, k * P:(k + 1) * P], ea_one_T[:, k, :], we_diag[:, :],
                                                            start=True, stop=True)
                                last.then_inc(e_done, 1)
                            for w in range(WINS):
                                pe.wait_ge(hot_set, WINS * g + w + 1)
                                if w or not isinstance(g, int) or g:
                                    pe.wait_ge(win_added, WINS * g + w)
                                for j in range(T):
                                    last = nc.tensor.matmul(ps_m_s[0:width, 0:WIDE], msg_s[:, j, 0:width], wide_hot[:, j, :],
                                                            start=(j == 0), stop=(j == T - 1))
                                last.then_inc(win_done, 1)
                        groups(pe, body)

            def node_values(c):
                moved, used = sem(f"moved{c}"), sem(f"used{c}")
                h_T_done, h_T_kept = sem(f"h_T_done{c}"), sem(f"h_T_kept{c}")
                own, var_in, std_out = sem(f"node_own{c}"), sem(f"var_in{c}"), sem(f"std_out{c}")
                done, kept = sem(f"values_done{c}"), sem(f"values_kept{c}")
                h = (None, x1_s, h1_s)[c]
                to = (x1_s, h1_s, y_s)[c]
                with nc.Block() as block:
                    @block.tensor
                    def _(pe):
                        for b in range(NB):
                            if b:
                                pe.wait_ge(used, b)
                            if c == 0:
                                nc.tensor.transpose(ps_t_s[0:NP, 0:MSG], sums_T[:, b * NP:(b + 1) * NP],
                                                    ident[0:MSG, 0:MSG]).then_inc(moved, 1)
                            else:
                                nc.tensor.transpose(ps_t_s[0:F, 0:NP], h[:, b, :], ident[0:NP, 0:NP]).then_inc(h_T_done, 1)
                                pe.wait_ge(h_T_kept, b + 1)
                                nc.tensor.matmul(ps_e_s[0:NP, 0:F], sums_T[0:F, b * NP:(b + 1) * NP],
                                                 wl_wr_T[:, c - 1, 0:F], start=True, stop=True)
                                nc.tensor.matmul(ps_e_s[0:NP, F:2 * F], hT_s[:, :],
                                                 wl_wr_T[:, c - 1, F:], start=True, stop=True).then_inc(moved, 1)

                    @block.scalar
                    def _(act):
                        if c != 1:
                            act.wait_ge(var_in, 1)
                            nc.scalar.activation(std_s[:, :], var_s[:, :], ACT.Sqrt, bias=eps_s[:, 0:1], scale=1.0 / F).then_inc(std_out, 1)

                    @block.sync
                    def _(sp):
                        sp.wait_ge(done, 1)
                        where = out if c == 2 else h_table
                        sp.dma_start(where.rearrange("(b p) f -> p b f", p=NP), to[:, :, :]).then_inc(kept, 16)
                        sp.wait_ge(kept, 16)

                    @block.vector
                    def _(dve):
                        steps_done = [0]

                        def after(ins):
                            steps_done[0] += 1
                            ins.then_inc(own, 1)
                            dve.wait_ge(own, steps_done[0])

                        for b in range(NB):
                            if c == 0:
                                dve.wait_ge(moved, b + 1)
                                nc.vector.tensor_scalar(rcnt_s[:, b:b + 1], ps_t_s[0:NP, F + HEADS:MSG], 1.0, None, ALU.max)
                                after(nc.vector.tensor_scalar(rz_s[:, b, :], ps_t_s[0:NP, F:F + HEADS], 1e-6, None, ALU.add))
                                after(nc.vector.reciprocal(rz_s[:, b, :], rz_s[:, b, :]))
                                nc.vector.tensor_tensor(
                                    y_s[:, b, :].rearrange("p (h d) -> p h d", d=HD),
                                    ps_t_s[0:NP, 0:F].rearrange("p (h d) -> p h d", d=HD),
                                    rz_s[:, b, :].rearrange("p (h a) -> p h a", a=1).to_broadcast([NP, HEADS, HD]),
                                    ALU.mult).then_inc(used, 1)
                            else:
                                dve.wait_ge(h_T_done, b + 1)
                                nc.vector.tensor_copy(hT_s[:, :], ps_t_s[0:F, 0:NP]).then_inc(h_T_kept, 1)
                                dve.wait_ge(moved, b + 1)
                                after(nc.vector.tensor_scalar(sq_s[:, b, :], ps_e_s[0:NP, 0:F], rcnt_s[:, b:b + 1], None, ALU.mult))
                                nc.vector.tensor_tensor(to[:, b, :], sq_s[:, b, :], ps_e_s[0:NP, F:2 * F], ALU.add).then_inc(used, 1)
                        dve.wait_ge(used, NB)
                        if c == 0:
                            after(nc.vector.reciprocal(rcnt_s[:, :], rcnt_s[:, :]))
                            nc.vector.memset(eps_s[:, :], EPS)
                            after(nc.vector.tensor_tensor(y_s[:, :, :], y_s[:, :, :], x_sb[:, :, :], ALU.add))
                        else:
                            after(nc.vector.tensor_tensor(to[:, :, :], to[:, :, :],
                                                          bias[0:NP, c - 1:c, :].to_broadcast([NP, NB, F]), ALU.add))
                            after(nc.vector.tensor_scalar(to[:, :, :], to[:, :, :], 0.0, None, ALU.max))
                            if c == 2:
                                after(nc.vector.tensor_tensor(y_s[:, :, :], y_s[:, :, :], x1_s[:, :, :], ALU.add))
                        if c != 1:
                            after(norm(dve, after, y_s, sq_s, mean_s, var_s, std_s, var_in, std_out, 1, to[:, :, :]))
                        after(nc.vector.memset(sums_T[:, :], 0.0))
                        nc.vector.nop().then_inc(done, 1)

            for c in range(3):
                segment_sums(c)
                node_values(c)
            g_ctx.close()
        tab_ctx.close()

        with nc.Else():
            counts_ctx = ExitStack()
            counts_T = sb(counts_ctx, "counts_T", [P, NB, NW], bf16, side="right")

            e_ctx = ExitStack()
            U = 4
            SL = 2
            src_now = sb(e_ctx, "src_now", [P, U, T], i32)
            kv = sb(e_ctx, "kv", [P, U, T, 2 * F])
            ea = sb(e_ctx, "ea", [P, SL, T, F])
            q_win = sb(e_ctx, "q_win", [W, SL, F])
            d_hot = sb(e_ctx, "d_hot", [P, U, T, W])
            d_hot_T = sb(e_ctx, "d_hot_T", [W, T, P])
            ea_T = sb(e_ctx, "ea_T", [P, T // 2, P])
            l_off = sb(e_ctx, "l_off", [P, T, P], f16)
            l_hot = sb(e_ctx, "l_hot", [P, T, P], bf16)
            k_hot = sb(e_ctx, "k_hot", [P, T, KEYS], bf16)
            kq = sb(e_ctx, "kq", [P, T, F])
            score = sb(e_ctx, "score", [P, T * HEADS])
            score_c = sb(e_ctx, "score_c", [P, T, HEADS])
            msg = sb(e_ctx, "msg", [P, SL, T, MSG])

            ps_dT = pb(e_ctx, "ps_dT", [P, 512])
            ps_eT = pb(e_ctx, "ps_eT", [P, 512])
            ps_eq = pb(e_ctx, "ps_eq", [P, 2, T, F])
            ps_sum = pb(e_ctx, "ps_sum", [P, 512])
            ps_cnt = pb(e_ctx, "ps_cnt", [P, SL, 2, 512])

            ea_arrived = [sem(f"ea_arrived{s}") for s in range(SL)]
            q_arrived = [sem(f"q_arrived{s}") for s in range(SL)]
            kv_arrived = [sem(f"kv_arrived{s}") for s in range(U)]
            src_ready = sem("src_ready")
            gathers_begun = sem("gathers_begun")
            ones_ready = sem("ones_ready")
            edges_zeroed = sem("edges_zeroed")
            transposed = sem("transposed")
            t_copied = sem("t_copied")
            eq_ready = sem("eq_ready")
            kq_done = sem("kq_done")
            eq_used = sem("eq_used")
            heads_done = sem("heads_done")
            clip_ready = sem("clip_ready")
            exp_ready = sem("exp_ready")
            msg_ready = sem("msg_ready")
            d_ready = sem("d_ready")
            hot_ready = sem("hot_ready")
            off_ready = sem("off_ready")
            place_ready = sem("place_ready")
            cnt_done = sem("cnt_done")
            cnt_copied = sem("cnt_copied")
            col_added = sem("col_added")
            sum_done = sem("sum_done")
            sum_added = sem("sum_added")

            ITER = NG // U

            def steps(eng, body, bases=None):
                def step(i):
                    found = [None] * U
                    if bases is not None:
                        _, found = nc.values_load_multi_w_load_instructions(
                            bases[0:1, bass.ds(U * i, U)], engines=[eng.engine], min_val=0, max_val=N - 1,
                            skip_runtime_bounds_check_because="targets are nodes, of which there are N")
                    for s in range(U):
                        body(i, s, found[s])

                step(0)
                with eng.Fori(1, ITER - 1) as i:
                    step(i)
                step(ITER - 1)

            def at(i, s, ahead):
                return i + (s + ahead) // U, (s + ahead) % U

            def exists(i, s, ahead):
                return not (isinstance(i, int) and not 0 <= U * i + s + ahead < NG)

            def turn(i, s):
                return U // SL * i + s // SL + 1

            with nc.Block() as block:
                @block.sync
                def _(sp):
                    def body(i, s, base):
                        g = U * i + s
                        if exists(i, s, -SL):
                            sp.wait_ge(transposed, g - SL + 1)
                        if isinstance(i, int) and g == NG - 1:
                            sp.dma_start(ea[0:TFULL, s % SL, :, :],
                                         edge_attr[g * GE:g * GE + TFULL * T, :].rearrange("(p j) f -> p j f", j=T)).then_inc(ea_arrived[s % SL], 16)
                            sp.dma_start(ea[TFULL:TFULL + 1, s % SL, 0:TREST, :],
                                         edge_attr[g * GE + TFULL * T:E, :].rearrange("(p j) f -> p j f", p=1)).then_inc(ea_arrived[s % SL], 16)
                        else:
                            sp.dma_start(ea[:, s % SL, :, :],
                                         edge_attr[bass.ds(g * GE, GE), :].rearrange("(p j) f -> p j f", j=T)).then_inc(ea_arrived[s % SL], 16)
                        if exists(i, s, -SL):
                            sp.wait_ge(eq_ready, g - SL + 1)
                        sp.dma_start(q_win[:, s % SL, :], q_table[bass.ds(base, W), :]).then_inc(q_arrived[s % SL], 16)
                    steps(sp, body, base_now)

                @block.gpsimd
                def _(pool):
                    nc.gpsimd.memset(counts_T[:, :, 0:1], 0.0).then_inc(edges_zeroed, 1)
                    nc.gpsimd.memset(counts_T[:, :, N:NW], 0.0).then_inc(edges_zeroed, 1)

                    def body(i, s, _):
                        g = U * i + s
                        pool.wait_ge(src_ready, g + 1)
                        if exists(i, s, -U):
                            pool.wait_ge(msg_ready, g - U + 1)
                        pool.sem_inc(gathers_begun, 1)
                        for j in range(T):
                            nc.gpsimd.indirect_dma_start(kv[:, s, j, :], None, kv_table[:, :],
                                                         bass.IndirectOffsetOnAxis(ap=src_now[:, s, j:j + 1], axis=0)
                                                         ).then_inc(kv_arrived[s], 16)
                    steps(pool, body)

                @block.scalar
                def _(act):
                    def take_sources(i, s):
                        g = U * i + s
                        nc.scalar.activation(src_now[:, s, :], src_i[:, bass.ds(g, 1), :].rearrange("p a j -> p (a j)"),
                                             ACT.Copy).then_inc(src_ready, 1)

                    def copy_transposed(i, s):
                        g = U * i + s
                        act.wait_ge(transposed, g + 1)
                        if exists(i, s, -1):
                            act.wait_ge(eq_ready, g)
                        nc.scalar.activation(d_hot_T[:, :, :].rearrange("p j e -> p (j e)"), ps_dT[0:W, :], ACT.Copy)
                        nc.scalar.activation(ea_T[:, :, :].rearrange("p j e -> p (j e)"), ps_eT[:, 0:T // 2 * P],
                                             ACT.Copy).then_inc(t_copied, 1)

                    def place_hots(i, s):
                        g = U * i + s
                        if exists(i, s, -1):
                            act.wait_ge(place_ready, g)
                        for j in range(T):
                            last = nc.scalar.activation(l_off[:, j, :], iota[:, 0:P], ACT.Abs,
                                                        bias=lo_tab[:, bass.ds(g, 1), j:j + 1].rearrange("p a j -> p (a j)"))
                        last.then_inc(off_ready, 1)
                        if exists(i, s, -1):
                            act.wait_ge(cnt_done, T * g)
                        act.wait_ge(off_ready, g + 1)
                        nc.scalar.activation(l_hot[:, :, :].rearrange("p j n -> p (j n)"), l_off[:, :, :].rearrange("p j n -> p (j n)"),
                                             ACT.Relu, bias=one[:, 0:1], scale=-1.0).then_inc(place_ready, 1)

                    for s in range(U):
                        take_sources(0, s)
                    place_hots(0, 0)
                    copy_transposed(0, 0)
                    copy_transposed(0, 1)
                    act.wait_ge(edges_zeroed, 2)

                    def body(i, s, base):
                        g = U * i + s
                        if exists(i, s, 1):
                            place_hots(*at(i, s, 1))
                        act.wait_ge(clip_ready, g + 1)
                        nc.scalar.activation(msg[:, s % SL, :, F:F + HEADS], score_c[:, :, :], ACT.Exp,
                                             scale=1.0 / HD ** 0.5).then_inc(exp_ready, 1)
                        if exists(i, s, U):
                            act.wait_ge(kv_arrived[s], 16 * T * (i + 1))
                            take_sources(i + 1, s)
                        act.wait_ge(cnt_done, T * (g + 1))
                        if exists(i, s, -1):
                            act.wait_ge(col_added, g)
                        for h in range(2):
                            d0 = 1 - h
                            last = nc.scalar.activation(
                                counts_T[:, :, bass.ds(base + (h * WH + d0), WH - d0)],
                                ps_cnt[:, s % SL, h, d0 * NB:WH * NB].rearrange("p (d b) -> p b d", b=NB), ACT.Copy)
                        last.then_inc(cnt_copied, 1)
                        if exists(i, s, 2):
                            copy_transposed(*at(i, s, 2))
                    steps(act, body, base_now)

                @block.vector
                def _(dve):
                    def targets(i, s):
                        g = U * i + s
                        nc.vector.tensor_tensor(
                            d_hot[:, s, :, :], iota[:, 0:W].rearrange("p (a w) -> p a w", a=1).to_broadcast([P, T, W]),
                            rel_tab[:, bass.ds(g, 1), :].rearrange("p a (j b) -> p (a j) b", b=1).to_broadcast([P, T, W]),
                            ALU.is_equal).then_inc(d_ready, 1)

                    def key_hot(i, s, j):
                        if exists(i, s, 0):
                            g = U * i + s
                            if exists(i, s, -1):
                                dve.wait_ge(cnt_done, T * g - T + j + 1)
                            nc.vector.tensor_scalar(k_hot[:, j, :], iota[:, :],
                                                    key_tab[:, bass.ds(g, 1), j:j + 1].rearrange("p a j -> p (a j)"),
                                                    None, ALU.is_equal).then_inc(hot_ready, 1)

                    def add_sums(i, s, base):
                        g = U * i + s
                        dve.wait_ge(sum_done, g + 1)
                        if exists(i, s, -1):
                            dve.wait_ge(sum_added, g)
                        window = sums_T[:, bass.ds(base, W)]
                        nc.vector.tensor_tensor(window, window, ps_sum[0:MSG, 0:W], ALU.add).then_inc(sum_added, 1)

                    def add_column(i, s, base):
                        g = U * i + s
                        dve.wait_ge(cnt_copied, g + 1)
                        if exists(i, s, -1):
                            dve.wait_ge(col_added, g)
                        column = counts_T[:, :, bass.ds(base, 1)].rearrange("p b a -> p (b a)")
                        nc.vector.tensor_tensor(column, column, ps_cnt[:, s % SL, 0, 0:NB], ALU.add).then_inc(col_added, 1)

                    for s in range(SL):
                        nc.vector.memset(msg[:, s, :, F + HEADS:], 1.0).then_inc(ones_ready, 1)
                    targets(0, 0)
                    targets(0, 1)
                    for j in range(T):
                        key_hot(0, 0, j)
                    dve.wait_ge(edges_zeroed, 1)

                    def body(i, s, base):
                        g = U * i + s
                        dve.wait_ge(eq_ready, g + 1)
                        dve.wait_ge(kv_arrived[s], 16 * T * (i + 1))
                        nc.vector.tensor_tensor(kq[:, :, :], kv[:, s, :, 0:F], ps_eq[:, 1, :, :], ALU.mult).then_inc(kq_done, 1)
                        if exists(i, s, 2):
                            targets(*at(i, s, 2))
                        dve.wait_ge(kq_done, g + 1)
                        nc.vector.tensor_tensor(kq[:, :, :], kq[:, :, :], ps_eq[:, 0, :, :], ALU.mult).then_inc(eq_used, 1)
                        if exists(i, s, -1):
                            add_sums(*at(i, s, -1), base)
                        dve.wait_ge(eq_used, g + 1)
                        nc.vector.reduce_sum(score[:, :], kq[:, :, :].rearrange("p j (h d) -> p (j h) d", d=HD), axis=X).then_inc(heads_done, 1)
                        if exists(i, s, -1):
                            add_column(*at(i, s, -1), base)
                        dve.wait_ge(heads_done, g + 1)
                        lim = 5.0 * HD ** 0.5
                        nc.vector.tensor_scalar(score_c[:, :, :].rearrange("p j h -> p (j h)"), score[:, :], lim, -lim,
                                                ALU.min, ALU.max).then_inc(clip_ready, 1)
                        for j in range(T):
                            key_hot(*at(i, s, 1), j)
                        dve.wait_ge(exp_ready, g + 1)
                        nc.vector.tensor_tensor(
                            msg[:, s % SL, :, 0:F].rearrange("p j (h d) -> p j h d", d=HD),
                            kv[:, s, :, F:].rearrange("p j (h d) -> p j h d", d=HD),
                            msg[:, s % SL, :, F:F + HEADS].rearrange("p j (h a) -> p j h a", a=1).to_broadcast([P, T, HEADS, HD]),
                            ALU.mult).then_inc(msg_ready, 1)
                    steps(dve, body, base_last)
                    base = dve.value_load(base_now[0:1, NG - 1:NG], min_val=0, max_val=N - 1)
                    add_sums(ITER - 1, U - 1, base)
                    add_column(ITER - 1, U - 1, base)

                @block.tensor
                def _(pe):
                    def transposes(i, s):
                        g = U * i + s
                        pe.wait_ge(d_ready, g + 1)
                        if exists(i, s, -1):
                            pe.wait_ge(t_copied, g)
                        if isinstance(i, int) and g == NG - 1:
                            pe.wait_ge(ea_arrived[s % SL], 16 * (turn(i, s) + 1))
                        else:
                            pe.wait_ge(ea_arrived[s % SL], 16 * turn(i, s))
                        for c in range(T // 2):
                            nc.tensor.transpose(ps_eT[:, c * P:(c + 1) * P],
                                                ea[:, s % SL, 2 * c:2 * c + 2, :].rearrange("p j f -> p (j f)"), ident[:, :])
                        for j in range(T):
                            last = nc.tensor.transpose(ps_dT[0:W, j * P:(j + 1) * P], d_hot[:, s, j, :], ident[:, :])
                        last.then_inc(transposed, 1)

                    def count(i, s):
                        g = U * i + s
                        if exists(i, s, -SL):
                            pe.wait_ge(cnt_copied, g - SL + 1)
                            pe.wait_ge(col_added, g - SL + 1)
                        pe.wait_ge(place_ready, g + 1)
                        for j in range(T):
                            pe.wait_ge(hot_ready, T * g + j + 1)
                            for h in range(2):
                                last = nc.tensor.matmul(ps_cnt[:, s % SL, h, 0:WH * NB], l_hot[:, j, :],
                                                        k_hot[:, j, h * WH * NB:(h + 1) * WH * NB],
                                                        start=(j == 0), stop=(j == T - 1))
                            last.then_inc(cnt_done, 1)

                    def project(i, s):
                        g = U * i + s
                        pe.wait_ge(t_copied, g + 1)
                        pe.wait_ge(q_arrived[s % SL], 16 * turn(i, s))
                        if exists(i, s, -1):
                            pe.wait_ge(eq_used, g)
                        for c in range(T // 2):
                            nc.tensor.matmul(ps_eq[:, 0, 2 * c:2 * c + 2, :].rearrange("p j f -> p (j f)"), ea_T[:, c, :], we_diag[:, :],
                                             start=True, stop=True)
                        for j in range(T):
                            last = nc.tensor.matmul(ps_eq[:, 1, j, :], d_hot_T[:, j, :], q_win[:, s % SL, :], start=True, stop=True)
                        last.then_inc(eq_ready, 1)

                    transposes(0, 0)
                    project(0, 0)
                    transposes(0, 1)
                    count(0, 0)
                    pe.wait_ge(ones_ready, SL)

                    def body(i, s, _):
                        g = U * i + s
                        if exists(i, s, 1):
                            project(*at(i, s, 1))
                        if exists(i, s, 2):
                            transposes(*at(i, s, 2))
                        if exists(i, s, 1):
                            count(*at(i, s, 1))
                        pe.wait_ge(msg_ready, g + 1)
                        if exists(i, s, -1):
                            pe.wait_ge(sum_added, g)
                        for j in range(T):
                            last = nc.tensor.matmul(ps_sum[0:MSG, 0:W], msg[:, s % SL, j, :], d_hot[:, s, j, :],
                                                    start=(j == 0), stop=(j == T - 1))
                        last.then_inc(sum_done, 1)
                    steps(pe, body)
            e_ctx.close()
            edge_ctx.close()

            n_ctx = ExitStack()
            y = sb(n_ctx, "y", [NP, NB, F])
            x1 = sb(n_ctx, "x1", [NP, NB, F])
            root = sb(n_ctx, "root", [NP, NB, F])
            part = sb(n_ctx, "part", [NP, 2, BB, F])
            x_again = sb(n_ctx, "x_again", [NP, NB, F])
            h1 = x_again
            sq = root
            split = sb(n_ctx, "split", [NP, NB, 3, F], bf16)
            h_T = sums_T[0:F, 0:N]
            rz = sb(n_ctx, "rz", [NP, NB, HEADS])
            rcnt = sb(n_ctx, "rcnt", [NP, NB])
            mean = sb(n_ctx, "mean", [NP, NB])
            var = sb(n_ctx, "var", [NP, NB])
            std = sb(n_ctx, "std", [NP, NB])
            eps = sb(n_ctx, "eps", [NP, 1])

            ps_a = pb(n_ctx, "ps_a", [P, 4, 512])
            ps_t = pb(n_ctx, "ps_t", [P, 2, 512])
            ps_g = pb(n_ctx, "ps_g", [P, 2, 512])
            SB = 512 // MSG
            SR = -(-NB // SB)
            PR = -(-NB // 2)
            parts_done = [sem("parts_done0"), sem("parts_done1")]

            sums_transposed = sem("sums_transposed")
            chain = sem("node_chain")
            eps_ready = sem("eps_ready")
            var_ready, std_ready = sem("var_ready"), sem("std_ready")
            h_ready = sem("h_ready")
            hT_done, hT_copied = sem("hT_done"), sem("hT_copied")
            g_done = sem("g_done")
            hi_ready = sem("hi_ready")
            rest_ready = sem("rest_ready")
            mid_ready = sem("mid_ready")
            lo_ready = sem("lo_ready")
            agg_done = sem("agg_done")
            agg_used = sem("agg_used")
            y_ready = sem("y_ready")
            x_arrived = sem("x_arrived")
            stored = sem("stored")

            with nc.Block() as block:
                @block.sync
                def _(sp):
                    sp.dma_start(x_again[:, :, :], x.rearrange("(b p) f -> p b f", p=NP)).then_inc(x_arrived, 16)
                    sp.wait_ge(y_ready, 1)
                    sp.dma_start(out.rearrange("(b p) f -> p b f", p=NP), y[:, :, :]).then_inc(stored, 16)
                    sp.wait_ge(stored, 16)

                @block.tensor
                def _(pe):
                    for b in range(NB):
                        t = nc.tensor.transpose(ps_a[0:NP, b // SB, b % SB * MSG:(b % SB + 1) * MSG],
                                                sums_T[:, b * NP:(b + 1) * NP], ident[0:MSG, 0:MSG])
                        if b % SB == SB - 1 or b == NB - 1:
                            t.then_inc(sums_transposed, 1)
                    for c in range(2):
                        h = (x1, h1)[c]
                        pe.wait_ge(h_ready, c + 1)

                        def products(r):
                            n = XG * c + r
                            pe.wait_ge(hT_copied, n + 1)
                            if n >= 2:
                                pe.wait_ge(lo_ready, n - 1)
                            for b in range(BB * r, min(BB * r + BB, NB)):
                                k = b - BB * r
                                last = nc.tensor.matmul(ps_g[0:NP, n % 2, k * 2 * F:(k + 1) * 2 * F],
                                                        h_T[:, b * NP:(b + 1) * NP], wl_wr_T[:, c, :], start=True, stop=True)
                            last.then_inc(g_done, 1)

                        for r in range(XG):
                            n = XG * c + r
                            if n >= 2:
                                pe.wait_ge(hT_copied, n - 1)
                            for b in range(BB * r, min(BB * r + BB, NB)):
                                k = b - BB * r
                                last = nc.tensor.transpose(ps_t[0:F, n % 2, k * NP:(k + 1) * NP], h[:, b, :], ident[0:NP, 0:NP])
                            last.then_inc(hT_done, 1)
                            if r:
                                products(r - 1)
                        products(XG - 1)
                        for q in range(PR):
                            n = PR * c + q
                            if n >= 4:
                                pe.wait_ge(agg_used, n - 3)
                            for b in range(2 * q, min(2 * q + 2, NB)):
                                for a in range(NB):
                                    if q == 0 and b == 0 and a % BB == 0:
                                        pe.wait_ge(lo_ready, XG * c + a // BB + 1)
                                        pe.wait_ge(mid_ready, XG * c + a // BB + 1)
                                    last = nc.tensor.matmul(ps_a[:, n % 4, b % 2 * 3 * F:(b % 2 + 1) * 3 * F],
                                                            counts_T[0:NP, a, b * NP:b * NP + P],
                                                            split[:, a, :, :].rearrange("p c f -> p (c f)"),
                                                            start=(a == 0), stop=(a == NB - 1))
                            last.then_inc(agg_done, 1)

                @block.scalar
                def _(act):
                    def root_of_variance(c):
                        act.wait_ge(var_ready, c + 1)
                        nc.scalar.activation(std[:, :], var[:, :], ACT.Sqrt, bias=eps[:, 0:1], scale=1.0 / F).then_inc(std_ready, 1)

                    act.wait_ge(eps_ready, 1)
                    root_of_variance(0)
                    for c in range(2):
                        def first_parts(r):
                            n = XG * c + r
                            b0, k = BB * r, min(BB, NB - BB * r)
                            act.wait_ge(g_done, n + 1)
                            if c and r == 0:
                                act.wait_ge(agg_done, PR)
                            nc.scalar.activation(split[:, b0:b0 + k, 0, :],
                                                 ps_g[0:NP, n % 2, 0:k * 2 * F].rearrange("p (k f) -> p k f", f=2 * F)[:, :, 0:F],
                                                 ACT.Copy).then_inc(hi_ready, 1)

                        def second_parts(r):
                            n = XG * c + r
                            b0, k = BB * r, min(BB, NB - BB * r)
                            act.wait_ge(rest_ready, n + 1)
                            nc.scalar.activation(split[:, b0:b0 + k, 1, :], part[:, n % 2, 0:k, :], ACT.Copy).then_inc(mid_ready, 1)

                        for r in range(XG + 2):
                            if r < XG:
                                n = XG * c + r
                                w = min(BB, NB - BB * r) * NP
                                act.wait_ge(hT_done, n + 1)
                                nc.scalar.activation(h_T[:, BB * r * NP:BB * r * NP + w], ps_t[0:F, n % 2, 0:w], ACT.Copy).then_inc(hT_copied, 1)
                            if r and r <= XG:
                                first_parts(r - 1)
                            if r >= 2:
                                second_parts(r - 2)
                    root_of_variance(1)

                @block.vector
                def _(dve):
                    steps_done = [0]

                    def after(ins):
                        steps_done[0] += 1
                        ins.then_inc(chain, 1)
                        dve.wait_ge(chain, steps_done[0])

                    nc.vector.memset(eps[:, :], EPS).then_inc(eps_ready, 1)
                    for q in range(SR):
                        b0, k = SB * q, min(SB, NB - SB * q)
                        dve.wait_ge(sums_transposed, q + 1)
                        sums = ps_a[0:NP, q, 0:k * MSG].rearrange("p (b m) -> p b m", m=MSG)
                        nc.vector.tensor_scalar(rcnt[:, b0:b0 + k], sums[:, :, F + HEADS], 1.0, None, ALU.max)
                        after(nc.vector.tensor_scalar(rz[:, b0:b0 + k, :], sums[:, :, F:F + HEADS], 1e-6, None, ALU.add))
                        after(nc.vector.reciprocal(rz[:, b0:b0 + k, :], rz[:, b0:b0 + k, :]))
                        for h in range(HEADS):
                            last = nc.vector.tensor_tensor(
                                y[:, b0:b0 + k, h * HD:(h + 1) * HD], sums[:, :, h * HD:(h + 1) * HD],
                                rz[:, b0:b0 + k, h:h + 1].to_broadcast([NP, k, HD]), ALU.mult)
                        after(last)
                    dve.wait_ge(x_arrived, 16)
                    after(nc.vector.tensor_tensor(y[:, :, :], y[:, :, :], x_again[:, :, :], ALU.add))
                    nc.vector.reciprocal(rcnt[:, :], rcnt[:, :])
                    norm(dve, after, y, sq, mean, var, std, var_ready, std_ready, 1, x1[:, :, :]).then_inc(h_ready, 1)

                    for c in range(2):
                        to = (h1, y)[c]
                        for r in range(XG):
                            n = XG * c + r
                            b0, k = BB * r, min(BB, NB - BB * r)
                            prod = ps_g[0:NP, n % 2, 0:k * 2 * F].rearrange("p (k f) -> p k f", f=2 * F)
                            dve.wait_ge(hi_ready, n + 1)
                            if n >= 2:
                                dve.wait_ge(mid_ready, n - 1)
                            nc.vector.tensor_tensor(part[:, n % 2, 0:k, :], prod[:, :, 0:F], split[:, b0:b0 + k, 0, :],
                                                    ALU.subtract).then_inc(rest_ready, 1)
                            nc.vector.tensor_tensor(root[:, b0:b0 + k, :], prod[:, :, F:],
                                                    bias[0:NP, c:c + 1, :].to_broadcast([NP, k, F]), ALU.add)
                            dve.wait_ge(mid_ready, n + 1)
                            nc.vector.tensor_tensor(split[:, b0:b0 + k, 2, :], part[:, n % 2, 0:k, :], split[:, b0:b0 + k, 1, :],
                                                    ALU.subtract).then_inc(lo_ready, 1)
                        for q in range(PR):
                            n = PR * c + q
                            b0, k = 2 * q, min(2, NB - 2 * q)
                            dve.wait_ge(agg_done, n + 1)
                            last = nc.vector.reduce_sum(to[:, b0:b0 + k, :],
                                                        ps_a[0:NP, n % 4, 0:k * 3 * F].rearrange("p (b c f) -> p b f c", c=3, f=F), axis=X)
                            last.then_inc(agg_used, 1)
                            dve.wait_ge(agg_used, n + 1)
                            for b in range(b0, b0 + k):
                                last = nc.vector.scalar_tensor_tensor(out=to[:, b, :], in0=to[:, b, :], scalar=rcnt[:, b:b + 1],
                                                                      in1=root[:, b, :], op0=ALU.mult, op1=ALU.add)
                            after(last)
                            last = nc.vector.tensor_scalar(to[:, b0:b0 + k, :], to[:, b0:b0 + k, :], 0.0, None, ALU.max)
                            after(last)
                        if c == 0:
                            nc.vector.nop().then_inc(h_ready, 1)
                    after(nc.vector.tensor_tensor(y[:, :, :], y[:, :, :], x1[:, :, :], ALU.add))
                    norm(dve, after, y, sq, mean, var, std, var_ready, std_ready, 2, y[:, :, :]).then_inc(y_ready, 1)
            n_ctx.close()
            counts_ctx.close()


_INS = ["x", "src", "dst", "edge_attr_64", "L0_gnn_Wq", "L0_gnn_Wk", "L0_gnn_We", "L0_gnn_Wv", "L1_gnn_W_l1",
        "L1_gnn_b1", "L1_gnn_W_r1", "L1_gnn_W_l2", "L1_gnn_b2", "L1_gnn_W_r2"]


def kernel(**inputs):
    import numpy as np
    import concourse.bacc as bacc
    from concourse import mybir
    from concourse.bass_utils import run_bass_kernel_spmd as run

    nc = bacc.Bacc("TRN2", target_bir_lowering=False, num_devices=1)
    arrays, args = {}, []
    for name in _INS:
        a = np.ascontiguousarray(inputs[name])
        arrays[f"in_{name}"] = a
        args.append(nc.dram_tensor(f"in_{name}", a.shape, mybir.dt.from_np(a.dtype), kind="ExternalInput").ap())
    n, f = inputs["x"].shape
    args.append(nc.dram_tensor("out_0", (n, f), mybir.dt.float32, kind="ExternalOutput").ap())
    gnn_kernel(nc, *args)
    return run(nc, [arrays], core_ids=[0]).results[0]["out_0"]
```

```python
import concourse.bass as bass
from concourse import mybir
from contextlib import ExitStack


def gnn_kernel(nc, x, src, dst, edge_attr, Wq, Wk, We, Wv, Wl1, b1, Wr1, Wl2, b2, Wr2, out):
    f32, bf16, f16, i32 = mybir.dt.float32, mybir.dt.bfloat16, mybir.dt.float16, mybir.dt.int32
    ALU = mybir.AluOpType
    ACT = mybir.ActivationFunctionType
    X = mybir.AxisListType.X

    N, F = x.shape
    E = src.shape[0]
    HEADS = 4
    HD = F // HEADS
    P = 128
    NB = 25
    NP = N // NB
    T = 4
    GE = P * T
    NG = -(-E // GE)
    TAIL = E - (NG - 1) * GE
    TFULL, TREST = TAIL // T, TAIL % T
    W = 40
    WH = W // 2
    KEYS = W * NB
    NW = N + W
    MSG = F + HEADS + 1
    FAR = 1 << 20
    DUP = 127
    MAGIC = 1.5 * 2.0 ** 23
    EPS = 1e-5
    BB = 4

    ctx = ExitStack()
    with ctx:
        def sb(stack, name, shape, dt=f32, side="left"):
            return stack.enter_context(nc.sbuf_tensor(name, shape, dt, side=side))

        def pb(stack, name, shape):
            return stack.enter_context(nc.psum_tensor(name, shape, f32))

        def sem(name):
            return ctx.enter_context(nc.semaphore(name))

        kv_table = nc.dram_tensor("kv_table", (N, 2 * F), f32, kind="Internal").ap()
        q_table = nc.dram_tensor("q_table", (NW, F), f32, kind="Internal").ap()

        ident = sb(ctx, "ident", [P, P])
        bias = sb(ctx, "bias", [P, 2, F])
        sums_T = sb(ctx, "sums_T", [P, NW])

        s_load, s_tload, s_next = sem("sources_loaded"), sem("targets_loaded"), sem("next_loaded")
        s_wload = sem("weights_loaded")
        s_xload, s_weload = [sem("x_loaded0"), sem("x_loaded1")], sem("we_loaded")
        s_pad = sem("padding_written")
        s_id = sem("identity_ready")
        s_rowsf = sem("rows_converted")
        s_checked = sem("rows_checked")
        s_odd = sem("irregularities_summed")
        s_idT = sem("index_transposed")
        s_base = sem("base_row_ready")
        s_bb = sem("base_broadcast")
        s_tab = sem("table_chain")
        s_iota = sem("iota_ready")
        s_wT, s_wc = sem("weights_transposed"), sem("weights_copied")
        s_xT, s_xc = sem("x_transposed"), sem("x_copied")
        s_proj, s_projc = sem("projected"), sem("projection_copied")
        kv_stored, q_stored = sem("kv_stored"), sem("q_stored")
        s_zero = sem("zeros_ready")
        s_weT = sem("we_transposed")
        s_nextf = sem("next_converted")
        s_warm = sem("warm_ready")
        s_pool = sem("check_chain")
        s_late = sem("checks_marked")

        edge_ctx = ExitStack()
        src_i = sb(edge_ctx, "src_i", [P, NG, T], i32)
        lo_tab = sb(edge_ctx, "lo_tab", [P, NG, T])
        one = sb(edge_ctx, "one", [P, 1])
        key_tab = sb(edge_ctx, "key_tab", [P, NG, T], f16)
        rel_tab = sb(edge_ctx, "rel_tab", [P, NG, T])
        odd = sb(edge_ctx, "odd", [1, 1], i32)
        base_now = sb(edge_ctx, "base_now", [1, NG], i32)
        base_last = sb(edge_ctx, "base_last", [1, NG + 1], i32)
        iota = sb(edge_ctx, "iota", [P, KEYS], f16)
        we_diag = sb(edge_ctx, "we_diag", [P, P])

        tab_ctx = ExitStack()
        rows_i = sb(tab_ctx, "rows_i", [NG, 2, GE], i32, side="right")
        next_i = sb(tab_ctx, "next_i", [NG, GE], i32, side="right")
        next_f = sb(tab_ctx, "next_f", [NG, GE], side="right")
        late = sb(tab_ctx, "late", [NG, 3, GE], side="right")
        irregular = sb(tab_ctx, "irregular", [NG, 2], side="right")
        ones_col = sb(tab_ctx, "ones_col", [P, 1], side="right")
        rows_f = sb(tab_ctx, "rows_f", [NG, 2, GE], side="right")
        src_f = sb(tab_ctx, "src_f", [P, NG, T], side="right")
        dst_f = sb(tab_ctx, "dst_f", [P, NG, T], side="right")
        hi_tab = sb(tab_ctx, "hi_tab", [P, NG, T], side="right")
        in_tab = sb(tab_ctx, "in_tab", [P, NG, T], side="right")
        iota_i = sb(tab_ctx, "iota_i", [P, KEYS], i32, side="right")
        ones_row = sb(tab_ctx, "ones_row", [1, P], side="right")
        x_sb = sb(tab_ctx, "x_sb", [NP, NB, F], side="right")
        w_kv = sb(tab_ctx, "w_kv", [2 * F, 2, F], side="right")
        w_q = sb(tab_ctx, "w_q", [F, 2, F], side="right")
        w_ee = sb(tab_ctx, "w_ee", [F, 2, F], side="right")
        PAIRS = -(-NB // 2)
        w_kvq_T = sb(tab_ctx, "w_kvq_T", [P, 2, 3 * F], side="right")
        x_T = sb(tab_ctx, "x_T", [P, PAIRS, NP], side="right")
        kvq = sb(tab_ctx, "kvq", [NP, NB, 3 * F], side="right")
        zeros = sb(tab_ctx, "zeros", [W, F], side="right")
        warm = sb(tab_ctx, "warm", [P, 512], bf16, side="right")

        ps_s = pb(tab_ctx, "ps_s", [P, 512])
        ps_d = pb(tab_ctx, "ps_d", [P, 512])
        ps_b = pb(tab_ctx, "ps_b", [P, 512])
        ps_w = pb(tab_ctx, "ps_w", [P, 512])
        ps_x = pb(tab_ctx, "ps_x", [P, 2, 512])
        ps_k = pb(tab_ctx, "ps_k", [P, 2, 512])
        XG = -(-NB // BB)
        XR = -(-PAIRS // 4)
        store_rounds = [(q, q + 2) for q in range(0, PAIRS - 3, 2)] + [(PAIRS - 3, PAIRS)]

        with nc.Block() as block:
            @block.sync
            def _(sp):
                for h, w in enumerate((Wk, Wv)):
                    sp.dma_start(w_kv[h * F:(h + 1) * F, :, :], w.rearrange("o (a f) -> o a f", a=1).to_broadcast([F, 2, F])).then_inc(s_wload, 16)
                sp.dma_start(w_q[:, :, :], Wq.rearrange("o (a f) -> o a f", a=1).to_broadcast([F, 2, F])).then_inc(s_wload, 16)
                for s, (i0, i1) in enumerate(((0, 8), (8, NB))):
                    sp.dma_start(x_sb[:, i0:i1, :], x.rearrange("(b p) f -> p b f", p=NP)[:, i0:i1, :]).then_inc(s_xload[s], 16)
                sp.wait_ge(s_pad, 1)
                sp.dma_start(rows_i[0:NG - 1, 0, :], src[0:(NG - 1) * GE].rearrange("(g e) -> g e", e=GE)).then_inc(s_load, 16)
                sp.dma_start(rows_i[NG - 1:NG, 0, 0:TAIL], src[(NG - 1) * GE:E].rearrange("(g e) -> g e", g=1)).then_inc(s_load, 16)
                sp.dma_start(w_ee[:, :, :], We.rearrange("o (a f) -> o a f", a=1).to_broadcast([F, 2, F])).then_inc(s_weload, 16)
                sp.wait_ge(s_zero, 1)
                sp.dma_start(q_table[N:NW, :], zeros[:, :]).then_inc(q_stored, 16)
                for r, (q0, q1) in enumerate(store_rounds):
                    i0, i1 = 2 * q0, min(2 * q1, NB)
                    sp.wait_ge(s_projc, q1)
                    sp.dma_start(kv_table.rearrange("(b p) f -> p b f", p=NP)[:, i0:i1, :],
                                 kvq[:, i0:i1, 0:2 * F]).then_inc(kv_stored, 16)
                    sp.dma_start(q_table[0:N, :].rearrange("(b p) f -> p b f", p=NP)[:, i0:i1, :],
                                 kvq[:, i0:i1, 2 * F:]).then_inc(q_stored, 16)

            @block.scalar
            def _(act):
                def keep_x(r):
                    k = min(4, PAIRS - 4 * r)
                    rows = P if 8 * r + 1 < NB else F
                    act.wait_ge(s_xT, r + 1)
                    nc.scalar.activation(x_T[0:rows, 4 * r:4 * r + k, :].rearrange("p b n -> p (b n)"), ps_x[0:rows, r % 2, 0:k * NP],
                                         ACT.Copy).then_inc(s_xc, 1)

                keep_x(0)
                for r in range(XR):
                    if r and r + 1 < XR:
                        keep_x(r + 1)
                    for q in range(4 * r, min(4 * r + 4, PAIRS)):
                        k = min(2, NB - 2 * q)
                        act.wait_ge(s_proj, q + 1)
                        nc.scalar.activation(kvq[:, 2 * q:2 * q + k, :].rearrange("p b f -> p (b f)"),
                                             ps_k[0:NP, q % 2, 0:k * 3 * F], ACT.Copy).then_inc(s_projc, 1)
                    if r == 0:
                        act.wait_ge(s_next, 32)
                        nc.scalar.activation(next_f[:, :], next_i[:, :], ACT.Copy).then_inc(s_nextf, 1)
                        keep_x(1)

            @block.gpsimd
            def _(pool):
                nc.gpsimd.memset(warm[:, :], 0.0).then_inc(s_warm, 1)
                nc.gpsimd.memset(ident[:, :], 0.0).then_inc(s_id, 1)
                nc.gpsimd.memset(zeros[:, :], 0.0).then_inc(s_zero, 1)
                pool.wait_ge(s_id, 1)
                nc.gpsimd.affine_select(out=ident[:, :], in_=ident[:, :], compare_op=ALU.not_equal, fill=1.0,
                                        base=0, pattern=[[-1, P]], channel_multiplier=1).then_inc(s_id, 1)
                pool.wait_ge(s_pad, 3)
                pool.dma_start(rows_i[0:NG - 1, 1, :], dst[0:(NG - 1) * GE].rearrange("(g e) -> g e", e=GE)).then_inc(s_tload, 16)
                pool.dma_start(rows_i[NG - 1:NG, 1, 0:TAIL], dst[(NG - 1) * GE:E].rearrange("(g e) -> g e", g=1)).then_inc(s_tload, 16)
                pool.dma_start(next_i[0:NG - 1, :],
                               dst[1:(NG - 1) * GE + 1].rearrange("(g e) -> g e", e=GE)).then_inc(s_next, 16)
                pool.dma_start(next_i[NG - 1:NG, 0:TAIL - 1],
                               dst[(NG - 1) * GE + 1:E].rearrange("(g e) -> g e", g=1)).then_inc(s_next, 16)
                nc.gpsimd.memset(ones_row[:, :], 1.0).then_inc(s_id, 1)
                nc.gpsimd.memset(ones_col[:, :], 1.0).then_inc(s_id, 1)
                nc.gpsimd.memset(we_diag[:, :], 0.0).then_inc(s_zero, 1)
                nc.gpsimd.iota(iota_i[:, :], [[1, KEYS]], base=0, channel_multiplier=0).then_inc(s_iota, 1)
                nc.gpsimd.memset(sums_T[:, :], 0.0).then_inc(s_zero, 1)
                targets = rows_f[:, 1, :]
                pool.wait_ge(s_rowsf, 2)
                nc.gpsimd.tensor_scalar(late[:, 0, :], targets, float(N - 1), None, ALU.min).then_inc(s_pool, 1)
                nc.gpsimd.tensor_tensor(late[:, 2, 0:GE - DUP], rows_f[:, 1, DUP:], rows_f[:, 1, 0:GE - DUP], ALU.subtract).then_inc(s_pool, 1)
                pool.wait_ge(s_nextf, 1)
                pool.wait_ge(s_pool, 1)
                nc.gpsimd.tensor_tensor(late[:, 0, :], next_f[:, :], late[:, 0, :], ALU.subtract).then_inc(s_pool, 1)
                pool.wait_ge(s_pool, 2)
                nc.gpsimd.tensor_scalar(late[:, 2, 0:GE - DUP], late[:, 2, 0:GE - DUP], 0.0, None, ALU.is_equal).then_inc(s_late, 1)
                pool.wait_ge(s_pool, 3)
                nc.gpsimd.tensor_scalar(late[:, 0, :], late[:, 0, :], 0.0, None, ALU.is_lt).then_inc(s_late, 1)

            @block.tensor
            def _(pe):
                def transpose_x(r):
                    if r >= 2:
                        pe.wait_ge(s_xc, r - 1)
                    for q in range(4 * r, min(4 * r + 4, PAIRS)):
                        k = min(2, NB - 2 * q)
                        t = nc.tensor.transpose(ps_x[0:k * F, r % 2, (q - 4 * r) * NP:(q - 4 * r + 1) * NP],
                                                x_sb[:, 2 * q:2 * q + k, :].rearrange("p b f -> p (b f)"), ident[0:NP, 0:NP])
                    t.then_inc(s_xT, 1)

                def project(r):
                    pe.wait_ge(s_xc, r + 1)
                    for q in range(4 * r, min(4 * r + 4, PAIRS)):
                        k = min(2, NB - 2 * q)
                        if q >= 2:
                            pe.wait_ge(s_projc, q - 1)
                        nc.tensor.matmul(ps_k[0:NP, q % 2, 0:k * 3 * F], x_T[0:k * F, q, :],
                                         w_kvq_T[0:k * F, 0:k, :].rearrange("p a f -> p (a f)"),
                                         start=True, stop=True).then_inc(s_proj, 1)

                def keep_busy(n):
                    for _ in range(n):
                        nc.tensor.matmul(ps_k[:, 1, :], warm[:, 0:P], warm[:, :], start=True, stop=True)

                pe.wait_ge(s_warm, 1)
                keep_busy(8)
                pe.wait_ge(s_id, 2)
                pe.wait_ge(s_wload, 16 * 3)
                nc.tensor.transpose(ps_w[:, 0:P], w_kv[:, :, :].rearrange("p a f -> p (a f)"), ident[:, :])
                nc.tensor.transpose(ps_w[:, P:P + F], w_q[:, :, :].rearrange("p a f -> p (a f)"), ident[0:F, 0:F]).then_inc(s_wT, 1)
                keep_busy(3)
                pe.wait_ge(s_xload[0], 16)
                transpose_x(0)
                pe.wait_ge(s_wc, 1)
                project(0)
                pe.wait_ge(s_xload[1], 16)
                transpose_x(1)
                pe.wait_ge(s_rowsf, 2)
                for c, ps in enumerate((ps_s, ps_d)):
                    for j in range(T):
                        nc.tensor.transpose(ps[:, j * NG:(j + 1) * NG], rows_f[:, c, j::T],
                                            ident[0:NG, 0:NG]).then_inc(s_idT, 1)
                transpose_x(2)
                project(1)
                pe.wait_ge(s_id, 4)
                pe.wait_ge(s_base, 1)
                nc.tensor.matmul(ps_b[:, 0:NG], ones_row[:, :], dst_f[0:1, :, 0],
                                 start=True, stop=True).then_inc(s_bb, 1)
                transpose_x(3)
                project(2)
                project(3)
                pe.wait_ge(s_weload, 16)
                nc.tensor.transpose(ps_w[:, P + F:2 * P], w_ee[:, :, :].rearrange("p a f -> p (a f)"), ident[0:F, 0:F]).then_inc(s_weT, 1)
                pe.wait_ge(s_weT, 2)
                pe.wait_ge(s_checked, 1)
                nc.tensor.matmul(ps_w[0:1, 0:1], irregular[:, 0:1], ones_col[0:NG, :], start=True, stop=True).then_inc(s_odd, 1)

            @block.vector
            def _(dve):
                steps = [0]

                def after(ins):
                    steps[0] += 1
                    ins.then_inc(s_tab, 1)
                    dve.wait_ge(s_tab, steps[0])

                nc.vector.memset(rows_i[:, 0, :], 0).then_inc(s_pad, 1)
                nc.vector.memset(rows_i[:, 1, :], FAR).then_inc(s_pad, 1)
                nc.vector.memset(next_i[:, :], N - 1).then_inc(s_pad, 1)
                after(nc.vector.memset(w_kvq_T[:, :, :], 0.0))
                dve.wait_ge(s_wT, 1)
                nc.vector.tensor_copy(w_kvq_T[0:F, 0, :], ps_w[0:F, 0:3 * F])
                nc.vector.tensor_copy(w_kvq_T[F:, 1, :], ps_w[F:, 0:3 * F]).then_inc(s_wc, 1)
                for c, loaded in enumerate((s_load, s_tload)):
                    dve.wait_ge(loaded, 32)
                    nc.vector.tensor_copy(rows_f[:, c, :], rows_i[:, c, :]).then_inc(s_rowsf, 1)
                dve.wait_ge(s_iota, 1)
                nc.vector.tensor_copy(iota[:, :], iota_i[:, :])
                dve.wait_ge(s_idT, T)
                after(nc.vector.tensor_copy(src_f[:, :, :], ps_s[:, 0:T * NG].rearrange("p (j g) -> p g j", j=T)))
                nc.vector.tensor_copy(src_i[:, :, :], src_f[:, :, :])
                dve.wait_ge(s_idT, 2 * T)
                nc.vector.tensor_copy(dst_f[:, :, :], ps_d[:, 0:T * NG].rearrange("p (j g) -> p g j", j=T)).then_inc(s_base, 1)
                dve.wait_ge(s_base, 1)
                nc.vector.tensor_copy(base_now[:, :], dst_f[0:1, :, 0])
                nc.vector.tensor_copy(base_last[:, 0:1], dst_f[0:1, 0, 0:1])
                nc.vector.tensor_copy(base_last[:, 1:NG + 1], dst_f[0:1, :, 0])

                after(nc.vector.tensor_scalar(hi_tab[:, :, :], src_f[:, :, :], 1.0 / NP, -(NP // 2) / NP, ALU.mult, ALU.add))
                after(nc.vector.tensor_scalar(hi_tab[:, :, :], hi_tab[:, :, :], MAGIC, -MAGIC, ALU.add, ALU.add))
                nc.vector.scalar_tensor_tensor(out=lo_tab[:, :, :], in0=hi_tab[:, :, :], scalar=float(NP),
                                               in1=src_f[:, :, :], op0=ALU.mult, op1=ALU.subtract)
                nc.vector.memset(one[:, :], 1.0)
                dve.wait_ge(s_bb, 1)
                after(nc.vector.tensor_tensor(rel_tab[:, :, :], dst_f[:, :, :],
                                              ps_b[:, 0:NG].rearrange("p (g a) -> p g a", a=1).to_broadcast([P, NG, T]), ALU.subtract))
                nc.vector.scalar_tensor_tensor(out=hi_tab[:, :, :], in0=rel_tab[:, :, :], scalar=float(NB),
                                               in1=hi_tab[:, :, :], op0=ALU.mult, op1=ALU.add)
                after(nc.vector.tensor_scalar(in_tab[:, :, :], rel_tab[:, :, :], float(W), None, ALU.is_lt))
                after(nc.vector.scalar_tensor_tensor(out=hi_tab[:, :, :], in0=hi_tab[:, :, :], scalar=1.0,
                                                     in1=in_tab[:, :, :], op0=ALU.add, op1=ALU.mult))
                nc.vector.tensor_scalar(key_tab[:, :, :], hi_tab[:, :, :], -1.0, None, ALU.add)
                dve.wait_ge(s_nextf, 1)
                nc.vector.tensor_scalar(late[:, 1, :], next_f[:, :], rows_f[:, 1, 0:1], float(W), ALU.subtract, ALU.is_ge).then_inc(s_late, 1)
                dve.wait_ge(s_late, 3)
                nc.vector.reduce_sum(irregular[:, 0:1], late[:, 0:2, :].rearrange("p a e -> p (a e)"), axis=X)
                after(nc.vector.reduce_sum(irregular[:, 1:2], late[:, 2, 0:GE - DUP], axis=X))
                after(nc.vector.tensor_tensor(irregular[:, 0:1], irregular[:, 0:1], irregular[:, 1:2], ALU.add))
                after(nc.vector.tensor_tensor(irregular[0:1, 0:1], irregular[0:1, 0:1], rows_f[0:1, 1, 0:1], ALU.add))
                nc.vector.nop().then_inc(s_checked, 1)
                dve.wait_ge(s_zero, 2)
                dve.wait_ge(s_weT, 1)
                nc.vector.tensor_copy(we_diag[0:F, 0:F], ps_w[0:F, P + F:2 * P])
                nc.vector.tensor_copy(we_diag[F:, F:], ps_w[F:, P + F:2 * P]).then_inc(s_weT, 1)
                dve.wait_ge(s_odd, 1)
                nc.vector.tensor_copy(odd[:, :], ps_w[0:1, 0:1])

        def norm(dve, after, y, sq, mean, var, std, var_ready, std_ready, n, to):
            def wide(a):
                return a.rearrange("p (b a) -> p b a", a=1).to_broadcast([NP, NB, F])

            after(nc.vector.reduce_sum(mean[:, :], y[:, :, :], axis=X))
            after(nc.vector.tensor_scalar(mean[:, :], mean[:, :], 1.0 / F, None, ALU.mult))
            after(nc.vector.tensor_tensor(y[:, :, :], y[:, :, :], wide(mean[:, :]), ALU.subtract))
            after(nc.vector.tensor_tensor(sq[:, :, :], y[:, :, :], y[:, :, :], ALU.mult))
            nc.vector.reduce_sum(var[:, :], sq[:, :, :], axis=X).then_inc(var_ready, 1)
            dve.wait_ge(std_ready, n)
            after(nc.vector.reciprocal(std[:, :], std[:, :]))
            return nc.vector.tensor_tensor(to, y[:, :, :], wide(std[:, :]), ALU.mult)

        is_odd = nc.values_load(odd[0:1, 0:1], min_val=0, max_val=1 << 24,
                                skip_runtime_bounds_check_because="only compared with 0")
        with nc.If(is_odd > 0):
            g_ctx = ExitStack()

            def g_sem(name):
                return g_ctx.enter_context(nc.semaphore(name))

            WINS = 7
            WIDE = -(-N // WINS)
            h_table = nc.dram_tensor("h_table", (N, F), f32, kind="Internal").ap()
            src_one = sb(g_ctx, "src_one", [P, T], i32)
            dst_one = sb(g_ctx, "dst_one", [P, T], i32)
            rows = sb(g_ctx, "rows", [P, T, 2 * F])
            q_rows = sb(g_ctx, "q_rows", [P, T, F])
            ea_one = sb(g_ctx, "ea_one", [P, T, F])
            ea_one_T = sb(g_ctx, "ea_one_T", [P, T // 2, P])
            part_s = sb(g_ctx, "part_s", [P, T, F])
            score_s = sb(g_ctx, "score_s", [P, T * HEADS])
            msg_s = sb(g_ctx, "msg_s", [P, T, MSG])
            wide_hot = sb(g_ctx, "wide_hot", [P, T, WIDE])
            y_s = sb(g_ctx, "y_s", [NP, NB, F])
            x1_s = sb(g_ctx, "x1_s", [NP, NB, F])
            h1_s = sb(g_ctx, "h1_s", [NP, NB, F])
            sq_s = sb(g_ctx, "sq_s", [NP, NB, F])
            hT_s = sb(g_ctx, "hT_s", [F, NP])
            rz_s = sb(g_ctx, "rz_s", [NP, NB, HEADS])
            rcnt_s = sb(g_ctx, "rcnt_s", [NP, NB])
            mean_s = sb(g_ctx, "mean_s", [NP, NB])
            var_s = sb(g_ctx, "var_s", [NP, NB])
            std_s = sb(g_ctx, "std_s", [NP, NB])
            eps_s = sb(g_ctx, "eps_s", [NP, 1])
            wl_wr_T = sb(g_ctx, "wl_wr_T", [F, 2, 2 * F])
            w_s = sb(g_ctx, "w_s", [2 * F, 2, F])
            ps_t_s, ps_e_s, ps_m_s = ps_s, ps_d, ps_b
            s_gw, s_gb, s_gT = g_sem("layer_weights_loaded"), g_sem("biases_loaded"), g_sem("layer_weights_transposed")

            with nc.Block() as block:
                @block.sync
                def _(sp):
                    sp.wait_ge(kv_stored, 16 * len(store_rounds))
                    sp.wait_ge(q_stored, 16 * (1 + len(store_rounds)))
                    for c, (wl, wr, b) in enumerate([(Wl1, Wr1, b1), (Wl2, Wr2, b2)]):
                        sp.dma_start(w_s[0:F, c, :], wl).then_inc(s_gw, 16)
                        sp.dma_start(w_s[F:, c, :], wr).then_inc(s_gw, 16)
                        sp.dma_start(bias[:, c, :], b.rearrange("(a f) -> a f", a=1).to_broadcast([P, F])).then_inc(s_gb, 16)
                    sp.wait_ge(s_gb, 32)

                @block.tensor
                def _(pe):
                    pe.wait_ge(s_gw, 64)
                    for c in range(2):
                        nc.tensor.transpose(ps_w[0:F, c * P:(c + 1) * P], w_s[:, c, :], ident[:, :]).then_inc(s_gT, 1)

                @block.vector
                def _(dve):
                    dve.wait_ge(s_gT, 2)
                    nc.vector.tensor_copy(wl_wr_T[:, :, :].rearrange("p a f -> p (a f)"), ps_w[0:F, 0:2 * P])

            def groups(eng, body):
                body(0)
                with eng.Fori(1, NG - 1) as g:
                    body(g)
                body(NG - 1)

            def segment_sums(c):
                idx_set, rows_in = g_sem(f"idx_set{c}"), g_sem(f"rows_in{c}")
                go, ea_in, ea_T_done = g_sem(f"go{c}"), g_sem(f"ea_in{c}"), g_sem(f"ea_T_done{c}")
                ea_T_kept, e_done = g_sem(f"ea_T_kept{c}"), g_sem(f"e_done{c}")
                own, scored, weighted = g_sem(f"own{c}"), g_sem(f"scored{c}"), g_sem(f"weighted{c}")
                hot_set, win_done, win_added = g_sem(f"hot_set{c}"), g_sem(f"win_done{c}"), g_sem(f"win_added{c}")
                width = MSG if c == 0 else F
                arrivals = 16 * T * (2 if c == 0 else 1)
                with nc.Block() as block:
                    @block.sync
                    def _(sp):
                        def body(g):
                            if not isinstance(g, int) or g:
                                sp.wait_ge(ea_T_done, g)
                            if isinstance(g, int) and g == NG - 1:
                                sp.dma_start(ea_one[0:TFULL, :, :],
                                             edge_attr[g * GE:g * GE + TFULL * T, :].rearrange("(p j) f -> p j f", j=T)).then_inc(ea_in, 16)
                                sp.dma_start(ea_one[TFULL:TFULL + 1, 0:TREST, :],
                                             edge_attr[g * GE + TFULL * T:E, :].rearrange("(p j) f -> p j f", p=1)).then_inc(ea_in, 16)
                            else:
                                sp.dma_start(ea_one[:, :, :],
                                             edge_attr[bass.ds(g * GE, GE), :].rearrange("(p j) f -> p j f", j=T)).then_inc(ea_in, 16)
                        if c == 0:
                            groups(sp, body)

                    @block.gpsimd
                    def _(pool):
                        def body(g):
                            pool.wait_ge(idx_set, g + 1)
                            pool.sem_inc(go, 1)
                            for j in range(T):
                                table, to = (kv_table, rows[:, j, :]) if c == 0 else (h_table, msg_s[:, j, 0:F])
                                nc.gpsimd.indirect_dma_start(to, None, table[:, :],
                                                             bass.IndirectOffsetOnAxis(ap=src_one[:, j:j + 1], axis=0)
                                                             ).then_inc(rows_in, 16)
                                if c == 0:
                                    nc.gpsimd.indirect_dma_start(q_rows[:, j, :], None, q_table[:, :],
                                                                 bass.IndirectOffsetOnAxis(ap=dst_one[:, j:j + 1], axis=0)
                                                                 ).then_inc(rows_in, 16)
                        groups(pool, body)

                    @block.scalar
                    def _(act):
                        def body(g):
                            act.wait_ge(ea_T_done, g + 1)
                            if not isinstance(g, int) or g:
                                act.wait_ge(e_done, g)
                            nc.scalar.activation(ea_one_T[:, :, :].rearrange("p j e -> p (j e)"), ps_t_s[:, 0:T // 2 * P],
                                                 ACT.Copy).then_inc(ea_T_kept, 1)
                            act.wait_ge(scored, g + 1)
                            nc.scalar.activation(msg_s[:, :, F:F + HEADS], score_s[:, :].rearrange("p (j h) -> p j h", h=HEADS),
                                                 ACT.Exp, scale=1.0 / HD ** 0.5).then_inc(weighted, 1)
                        if c == 0:
                            groups(act, body)

                    @block.vector
                    def _(dve):
                        OWN = 3 if c == 0 else 0

                        def body(g):
                            first = isinstance(g, int) and g == 0
                            nc.vector.tensor_copy(src_one[:, :], src_i[:, bass.ds(g, 1), :].rearrange("p a j -> p (a j)"))
                            nc.vector.tensor_scalar(dst_one[:, :], dst_f[:, bass.ds(g, 1), :].rearrange("p a j -> p (a j)"),
                                                    float(N - 1), None, ALU.min).then_inc(idx_set, 1)
                            dve.wait_ge(rows_in, arrivals * (g + 1) if isinstance(g, int) else g * arrivals + arrivals)
                            if c == 0:
                                nc.vector.tensor_tensor(part_s[:, :, :], rows[:, :, 0:F], q_rows[:, :, :], ALU.mult).then_inc(own, 1)
                                dve.wait_ge(own, OWN * g + 1)
                                dve.wait_ge(e_done, g + 1)
                                nc.vector.tensor_tensor(part_s[:, :, :], part_s[:, :, :],
                                                        ps_e_s[:, 0:T * F].rearrange("p (j f) -> p j f", f=F), ALU.mult).then_inc(own, 1)
                                dve.wait_ge(own, OWN * g + 2)
                                nc.vector.reduce_sum(score_s[:, :], part_s[:, :, :].rearrange("p j (h d) -> p (j h) d", d=HD), axis=X).then_inc(own, 1)
                                dve.wait_ge(own, OWN * g + 3)
                                lim = 5.0 * HD ** 0.5
                                nc.vector.tensor_scalar(score_s[:, :], score_s[:, :], lim, -lim, ALU.min, ALU.max).then_inc(scored, 1)
                                dve.wait_ge(weighted, g + 1)
                                nc.vector.tensor_tensor(
                                    msg_s[:, :, 0:F].rearrange("p j (h d) -> p j h d", d=HD),
                                    rows[:, :, F:].rearrange("p j (h d) -> p j h d", d=HD),
                                    msg_s[:, :, F:F + HEADS].rearrange("p j (h a) -> p j h a", a=1).to_broadcast([P, T, HEADS, HD]),
                                    ALU.mult)
                            for w in range(WINS):
                                for j in range(T):
                                    last = nc.vector.tensor_scalar(wide_hot[:, j, :], iota[:, 0:WIDE], float(w * WIDE),
                                                                   dst_f[:, bass.ds(g, 1), j:j + 1].rearrange("p a j -> p (a j)"),
                                                                   ALU.add, ALU.is_equal)
                                last.then_inc(hot_set, 1)
                                dve.wait_ge(win_done, WINS * g + w + 1)
                                if not first:
                                    dve.wait_ge(win_added, WINS * g - WINS + w + 1)
                                window = sums_T[0:width, w * WIDE:(w + 1) * WIDE]
                                nc.vector.tensor_tensor(window, window, ps_m_s[0:width, 0:WIDE], ALU.add).then_inc(win_added, 1)

                        if c == 0:
                            nc.vector.memset(msg_s[:, :, F + HEADS:], 1.0)
                        groups(dve, body)

                    @block.tensor
                    def _(pe):
                        def body(g):
                            if c == 0:
                                if isinstance(g, int) and g == NG - 1:
                                    pe.wait_ge(ea_in, 16 * (g + 2))
                                else:
                                    pe.wait_ge(ea_in, 16 * g + 16)
                                for k in range(T // 2):
                                    last = nc.tensor.transpose(ps_t_s[:, k * P:(k + 1) * P],
                                                               ea_one[:, 2 * k:2 * k + 2, :].rearrange("p j f -> p (j f)"), ident[:, :])
                                last.then_inc(ea_T_done, 1)
                                pe.wait_ge(ea_T_kept, g + 1)
                                for k in range(T // 2):
                                    last = nc.tensor.matmul(ps_e_s[:, k * P:(k + 1) * P], ea_one_T[:, k, :], we_diag[:, :],
                                                            start=True, stop=True)
                                last.then_inc(e_done, 1)
                            for w in range(WINS):
                                pe.wait_ge(hot_set, WINS * g + w + 1)
                                if w or not isinstance(g, int) or g:
                                    pe.wait_ge(win_added, WINS * g + w)
                                for j in range(T):
                                    last = nc.tensor.matmul(ps_m_s[0:width, 0:WIDE], msg_s[:, j, 0:width], wide_hot[:, j, :],
                                                            start=(j == 0), stop=(j == T - 1))
                                last.then_inc(win_done, 1)
                        groups(pe, body)

            def node_values(c):
                moved, used = g_sem(f"moved{c}"), g_sem(f"used{c}")
                h_T_done, h_T_kept = g_sem(f"h_T_done{c}"), g_sem(f"h_T_kept{c}")
                own, var_in, std_out = g_sem(f"node_own{c}"), g_sem(f"var_in{c}"), g_sem(f"std_out{c}")
                done, kept = g_sem(f"values_done{c}"), g_sem(f"values_kept{c}")
                h = (None, x1_s, h1_s)[c]
                to = (x1_s, h1_s, y_s)[c]
                with nc.Block() as block:
                    @block.tensor
                    def _(pe):
                        for b in range(NB):
                            if b:
                                pe.wait_ge(used, b)
                            if c == 0:
                                nc.tensor.transpose(ps_t_s[0:NP, 0:MSG], sums_T[0:MSG, b * NP:(b + 1) * NP],
                                                    ident[0:MSG, 0:MSG]).then_inc(moved, 1)
                            else:
                                nc.tensor.transpose(ps_t_s[0:F, 0:NP], h[:, b, :], ident[0:NP, 0:NP]).then_inc(h_T_done, 1)
                                pe.wait_ge(h_T_kept, b + 1)
                                nc.tensor.matmul(ps_e_s[0:NP, 0:F], sums_T[0:F, b * NP:(b + 1) * NP],
                                                 wl_wr_T[:, c - 1, 0:F], start=True, stop=True)
                                nc.tensor.matmul(ps_e_s[0:NP, F:2 * F], hT_s[:, :],
                                                 wl_wr_T[:, c - 1, F:], start=True, stop=True).then_inc(moved, 1)

                    @block.scalar
                    def _(act):
                        if c != 1:
                            act.wait_ge(var_in, 1)
                            nc.scalar.activation(std_s[:, :], var_s[:, :], ACT.Sqrt, bias=eps_s[:, 0:1], scale=1.0 / F).then_inc(std_out, 1)

                    @block.sync
                    def _(sp):
                        sp.wait_ge(done, 1)
                        where = out if c == 2 else h_table
                        sp.dma_start(where.rearrange("(b p) f -> p b f", p=NP), to[:, :, :]).then_inc(kept, 16)
                        sp.wait_ge(kept, 16)

                    @block.vector
                    def _(dve):
                        steps_done = [0]

                        def after(ins):
                            steps_done[0] += 1
                            ins.then_inc(own, 1)
                            dve.wait_ge(own, steps_done[0])

                        for b in range(NB):
                            if c == 0:
                                dve.wait_ge(moved, b + 1)
                                nc.vector.tensor_scalar(rcnt_s[:, b:b + 1], ps_t_s[0:NP, F + HEADS:MSG], 1.0, None, ALU.max)
                                after(nc.vector.tensor_scalar(rz_s[:, b, :], ps_t_s[0:NP, F:F + HEADS], 1e-6, None, ALU.add))
                                after(nc.vector.reciprocal(rz_s[:, b, :], rz_s[:, b, :]))
                                nc.vector.tensor_tensor(
                                    y_s[:, b, :].rearrange("p (h d) -> p h d", d=HD),
                                    ps_t_s[0:NP, 0:F].rearrange("p (h d) -> p h d", d=HD),
                                    rz_s[:, b, :].rearrange("p (h a) -> p h a", a=1).to_broadcast([NP, HEADS, HD]),
                                    ALU.mult).then_inc(used, 1)
                            else:
                                dve.wait_ge(h_T_done, b + 1)
                                nc.vector.tensor_copy(hT_s[:, :], ps_t_s[0:F, 0:NP]).then_inc(h_T_kept, 1)
                                dve.wait_ge(moved, b + 1)
                                after(nc.vector.tensor_scalar(sq_s[:, b, :], ps_e_s[0:NP, 0:F], rcnt_s[:, b:b + 1], None, ALU.mult))
                                nc.vector.tensor_tensor(to[:, b, :], sq_s[:, b, :], ps_e_s[0:NP, F:2 * F], ALU.add).then_inc(used, 1)
                        dve.wait_ge(used, NB)
                        if c == 0:
                            after(nc.vector.reciprocal(rcnt_s[:, :], rcnt_s[:, :]))
                            nc.vector.memset(eps_s[:, :], EPS)
                            after(nc.vector.tensor_tensor(y_s[:, :, :], y_s[:, :, :], x_sb[:, :, :], ALU.add))
                        else:
                            after(nc.vector.tensor_tensor(to[:, :, :], to[:, :, :],
                                                          bias[0:NP, c - 1:c, :].to_broadcast([NP, NB, F]), ALU.add))
                            after(nc.vector.tensor_scalar(to[:, :, :], to[:, :, :], 0.0, None, ALU.max))
                            if c == 2:
                                after(nc.vector.tensor_tensor(y_s[:, :, :], y_s[:, :, :], x1_s[:, :, :], ALU.add))
                        if c != 1:
                            after(norm(dve, after, y_s, sq_s, mean_s, var_s, std_s, var_in, std_out, 1, to[:, :, :]))
                        after(nc.vector.memset(sums_T[:, :], 0.0))
                        nc.vector.nop().then_inc(done, 1)

            for c in range(3):
                segment_sums(c)
                node_values(c)
            g_ctx.close()
        tab_ctx.close()

        with nc.Else():
            counts_ctx = ExitStack()
            counts_T = sb(counts_ctx, "counts_T", [P, NB, NW], f16, side="right")

            e_ctx = ExitStack()
            U = 4
            SL = 2
            src_now = sb(e_ctx, "src_now", [P, U, T], i32)
            kv = sb(e_ctx, "kv", [P, U, T, 2 * F])
            ea = sb(e_ctx, "ea", [P, SL, T, F])
            q_win = sb(e_ctx, "q_win", [W, SL, F])
            d_hot = sb(e_ctx, "d_hot", [P, U, T, W])
            d_hot_T = sb(e_ctx, "d_hot_T", [W, T, P])
            ea_T = sb(e_ctx, "ea_T", [P, T // 2, P])
            l_off = sb(e_ctx, "l_off", [P, T, P], f16)
            l_hot = sb(e_ctx, "l_hot", [P, T, P], bf16)
            k_hot = sb(e_ctx, "k_hot", [P, T, KEYS], bf16)
            kq = sb(e_ctx, "kq", [P, T, F])
            score = sb(e_ctx, "score", [P, T * HEADS])
            score_c = sb(e_ctx, "score_c", [P, T, HEADS])
            msg = sb(e_ctx, "msg", [P, SL, T, MSG])

            ps_dT = pb(e_ctx, "ps_dT", [P, 512])
            ps_eT = pb(e_ctx, "ps_eT", [P, 512])
            ps_eq = pb(e_ctx, "ps_eq", [P, 2, T, F])
            ps_sum = pb(e_ctx, "ps_sum", [P, 512])
            ps_cnt = pb(e_ctx, "ps_cnt", [P, SL, 2, 512])

            ea_arrived = [sem(f"ea_arrived{s}") for s in range(SL)]
            q_arrived = [sem(f"q_arrived{s}") for s in range(SL)]
            kv_arrived = [sem(f"kv_arrived{s}") for s in range(U)]
            src_ready = sem("src_ready")
            gathers_begun = sem("gathers_begun")
            ones_ready = sem("ones_ready")
            edges_zeroed = sem("edges_zeroed")
            transposed = sem("transposed")
            t_copied = sem("t_copied")
            eq_ready = sem("eq_ready")
            kq_done = sem("kq_done")
            eq_used = sem("eq_used")
            heads_done = sem("heads_done")
            clip_ready = sem("clip_ready")
            exp_ready = sem("exp_ready")
            msg_ready = sem("msg_ready")
            d_ready = sem("d_ready")
            hot_ready = sem("hot_ready")
            off_ready = sem("off_ready")
            place_ready = sem("place_ready")
            cnt_done = sem("cnt_done")
            cnt_copied = sem("cnt_copied")
            col_added = sem("col_added")
            sum_done = sem("sum_done")
            sum_added = sem("sum_added")

            ITER = NG // U

            def steps(eng, body, bases=None):
                def step(i):
                    found = [None] * U
                    if bases is not None:
                        _, found = nc.values_load_multi_w_load_instructions(
                            bases[0:1, bass.ds(U * i, U)], engines=[eng.engine], min_val=0, max_val=N - 1,
                            skip_runtime_bounds_check_because="targets are nodes, of which there are N")
                    for s in range(U):
                        body(i, s, found[s])

                step(0)
                with eng.Fori(1, ITER - 1) as i:
                    step(i)
                step(ITER - 1)

            def at(i, s, ahead):
                return i + (s + ahead) // U, (s + ahead) % U

            def exists(i, s, ahead):
                return not (isinstance(i, int) and not 0 <= U * i + s + ahead < NG)

            def turn(i, s):
                return U // SL * i + s // SL + 1

            with nc.Block() as block:
                @block.sync
                def _(sp):
                    def body(i, s, base):
                        g = U * i + s
                        if exists(i, s, -SL):
                            sp.wait_ge(transposed, g - SL + 1)
                        if isinstance(i, int) and g == NG - 1:
                            sp.dma_start(ea[0:TFULL, s % SL, :, :],
                                         edge_attr[g * GE:g * GE + TFULL * T, :].rearrange("(p j) f -> p j f", j=T)).then_inc(ea_arrived[s % SL], 16)
                            sp.dma_start(ea[TFULL:TFULL + 1, s % SL, 0:TREST, :],
                                         edge_attr[g * GE + TFULL * T:E, :].rearrange("(p j) f -> p j f", p=1)).then_inc(ea_arrived[s % SL], 16)
                        else:
                            sp.dma_start(ea[:, s % SL, :, :],
                                         edge_attr[bass.ds(g * GE, GE), :].rearrange("(p j) f -> p j f", j=T)).then_inc(ea_arrived[s % SL], 16)
                        if exists(i, s, -SL):
                            sp.wait_ge(eq_ready, g - SL + 1)
                        sp.dma_start(q_win[:, s % SL, :], q_table[bass.ds(base, W), :]).then_inc(q_arrived[s % SL], 16)
                    sp.wait_ge(q_stored, 16 * (1 + len(store_rounds)))
                    steps(sp, body, base_now)

                @block.gpsimd
                def _(pool):
                    def body(i, s, _):
                        g = U * i + s
                        pool.wait_ge(src_ready, g + 1)
                        if exists(i, s, -U):
                            pool.wait_ge(msg_ready, g - U + 1)
                        pool.sem_inc(gathers_begun, 1)
                        for j in range(T):
                            nc.gpsimd.indirect_dma_start(kv[:, s, j, :], None, kv_table[:, :],
                                                         bass.IndirectOffsetOnAxis(ap=src_now[:, s, j:j + 1], axis=0)
                                                         ).then_inc(kv_arrived[s], 16)
                    pool.wait_ge(kv_stored, 16 * len(store_rounds))
                    steps(pool, body)

                @block.scalar
                def _(act):
                    def take_sources(i, s):
                        g = U * i + s
                        nc.scalar.activation(src_now[:, s, :], src_i[:, bass.ds(g, 1), :].rearrange("p a j -> p (a j)"),
                                             ACT.Copy).then_inc(src_ready, 1)

                    def copy_transposed(i, s):
                        g = U * i + s
                        act.wait_ge(transposed, g + 1)
                        if exists(i, s, -1):
                            act.wait_ge(eq_ready, g)
                        nc.scalar.activation(d_hot_T[:, :, :].rearrange("p j e -> p (j e)"), ps_dT[0:W, :], ACT.Copy)
                        nc.scalar.activation(ea_T[:, :, :].rearrange("p j e -> p (j e)"), ps_eT[:, 0:T // 2 * P],
                                             ACT.Copy).then_inc(t_copied, 1)

                    def place_hots(i, s):
                        g = U * i + s
                        if exists(i, s, -1):
                            act.wait_ge(place_ready, g)
                        for j in range(T):
                            last = nc.scalar.activation(l_off[:, j, :], iota[:, 0:P], ACT.Abs,
                                                        bias=lo_tab[:, bass.ds(g, 1), j:j + 1].rearrange("p a j -> p (a j)"))
                        last.then_inc(off_ready, 1)
                        if exists(i, s, -1):
                            act.wait_ge(cnt_done, T * g)
                        act.wait_ge(off_ready, g + 1)
                        nc.scalar.activation(l_hot[:, :, :].rearrange("p j n -> p (j n)"), l_off[:, :, :].rearrange("p j n -> p (j n)"),
                                             ACT.Relu, bias=one[:, 0:1], scale=-1.0).then_inc(place_ready, 1)

                    for s in range(U):
                        take_sources(0, s)
                    place_hots(0, 0)
                    copy_transposed(0, 0)
                    copy_transposed(0, 1)
                    act.wait_ge(edges_zeroed, 2)

                    def body(i, s, base):
                        g = U * i + s
                        if exists(i, s, 1):
                            place_hots(*at(i, s, 1))
                        act.wait_ge(clip_ready, g + 1)
                        nc.scalar.activation(msg[:, s % SL, :, F:F + HEADS], score_c[:, :, :], ACT.Exp,
                                             scale=1.0 / HD ** 0.5).then_inc(exp_ready, 1)
                        if exists(i, s, U):
                            act.wait_ge(kv_arrived[s], 16 * T * (i + 1))
                            take_sources(i + 1, s)
                        act.wait_ge(cnt_done, T * (g + 1))
                        if exists(i, s, -1):
                            act.wait_ge(col_added, g)
                        for h in range(2):
                            d0 = 1 - h
                            last = nc.scalar.activation(
                                counts_T[:, :, bass.ds(base + (h * WH + d0), WH - d0)],
                                ps_cnt[:, s % SL, h, d0 * NB:WH * NB].rearrange("p (d b) -> p b d", b=NB), ACT.Copy)
                        last.then_inc(cnt_copied, 1)
                        if exists(i, s, 2):
                            copy_transposed(*at(i, s, 2))
                    steps(act, body, base_now)

                @block.vector
                def _(dve):
                    def targets(i, s):
                        g = U * i + s
                        nc.vector.tensor_tensor(
                            d_hot[:, s, :, :], iota[:, 0:W].rearrange("p (a w) -> p a w", a=1).to_broadcast([P, T, W]),
                            rel_tab[:, bass.ds(g, 1), :].rearrange("p a (j b) -> p (a j) b", b=1).to_broadcast([P, T, W]),
                            ALU.is_equal).then_inc(d_ready, 1)

                    def key_hot(i, s, j):
                        if exists(i, s, 0):
                            g = U * i + s
                            if exists(i, s, -1):
                                dve.wait_ge(cnt_done, T * g - T + j + 1)
                            nc.vector.tensor_scalar(k_hot[:, j, :], iota[:, :],
                                                    key_tab[:, bass.ds(g, 1), j:j + 1].rearrange("p a j -> p (a j)"),
                                                    None, ALU.is_equal).then_inc(hot_ready, 1)

                    def add_sums(i, s, base):
                        g = U * i + s
                        dve.wait_ge(sum_done, g + 1)
                        if exists(i, s, -1):
                            dve.wait_ge(sum_added, g)
                        window = sums_T[0:MSG, bass.ds(base, W)]
                        nc.vector.tensor_tensor(window, window, ps_sum[0:MSG, 0:W], ALU.add).then_inc(sum_added, 1)

                    def add_column(i, s, base):
                        g = U * i + s
                        dve.wait_ge(cnt_copied, g + 1)
                        if exists(i, s, -1):
                            dve.wait_ge(col_added, g)
                        column = counts_T[:, :, bass.ds(base, 1)].rearrange("p b a -> p (b a)")
                        nc.vector.tensor_tensor(column, column, ps_cnt[:, s % SL, 0, 0:NB], ALU.add).then_inc(col_added, 1)

                    for s in range(SL):
                        nc.vector.memset(msg[:, s, :, F + HEADS:], 1.0).then_inc(ones_ready, 1)
                    targets(0, 0)
                    targets(0, 1)
                    for j in range(T):
                        key_hot(0, 0, j)
                    dve.wait_ge(kv_stored, 16 * len(store_rounds))
                    dve.wait_ge(q_stored, 16 * (1 + len(store_rounds)))
                    nc.vector.memset(counts_T[:, :, 0:1], 0.0).then_inc(edges_zeroed, 1)
                    nc.vector.memset(counts_T[:, :, N:NW], 0.0).then_inc(edges_zeroed, 1)
                    dve.wait_ge(edges_zeroed, 2)

                    def body(i, s, base):
                        g = U * i + s
                        dve.wait_ge(eq_ready, g + 1)
                        dve.wait_ge(kv_arrived[s], 16 * T * (i + 1))
                        nc.vector.tensor_tensor(kq[:, :, :], kv[:, s, :, 0:F], ps_eq[:, 1, :, :], ALU.mult).then_inc(kq_done, 1)
                        if exists(i, s, 2):
                            targets(*at(i, s, 2))
                        dve.wait_ge(kq_done, g + 1)
                        nc.vector.tensor_tensor(kq[:, :, :], kq[:, :, :], ps_eq[:, 0, :, :], ALU.mult).then_inc(eq_used, 1)
                        dve.wait_ge(eq_used, g + 1)
                        nc.vector.reduce_sum(score[:, :], kq[:, :, :].rearrange("p j (h d) -> p (j h) d", d=HD), axis=X).then_inc(heads_done, 1)
                        if exists(i, s, -1):
                            add_column(*at(i, s, -1), base)
                        dve.wait_ge(heads_done, g + 1)
                        lim = 5.0 * HD ** 0.5
                        nc.vector.tensor_scalar(score_c[:, :, :].rearrange("p j h -> p (j h)"), score[:, :], lim, -lim,
                                                ALU.min, ALU.max).then_inc(clip_ready, 1)
                        for j in range(T):
                            key_hot(*at(i, s, 1), j)
                        if exists(i, s, -1):
                            add_sums(*at(i, s, -1), base)
                        dve.wait_ge(exp_ready, g + 1)
                        nc.vector.tensor_tensor(
                            msg[:, s % SL, :, 0:F].rearrange("p j (h d) -> p j h d", d=HD),
                            kv[:, s, :, F:].rearrange("p j (h d) -> p j h d", d=HD),
                            msg[:, s % SL, :, F:F + HEADS].rearrange("p j (h a) -> p j h a", a=1).to_broadcast([P, T, HEADS, HD]),
                            ALU.mult).then_inc(msg_ready, 1)
                    steps(dve, body, base_last)
                    base = dve.value_load(base_now[0:1, NG - 1:NG], min_val=0, max_val=N - 1)
                    add_sums(ITER - 1, U - 1, base)
                    add_column(ITER - 1, U - 1, base)

                @block.tensor
                def _(pe):
                    def transposes(i, s):
                        g = U * i + s
                        pe.wait_ge(d_ready, g + 1)
                        if exists(i, s, -1):
                            pe.wait_ge(t_copied, g)
                        if isinstance(i, int) and g == NG - 1:
                            pe.wait_ge(ea_arrived[s % SL], 16 * (turn(i, s) + 1))
                        else:
                            pe.wait_ge(ea_arrived[s % SL], 16 * turn(i, s))
                        for c in range(T // 2):
                            nc.tensor.transpose(ps_eT[:, c * P:(c + 1) * P],
                                                ea[:, s % SL, 2 * c:2 * c + 2, :].rearrange("p j f -> p (j f)"), ident[:, :])
                        for j in range(T):
                            last = nc.tensor.transpose(ps_dT[0:W, j * P:(j + 1) * P], d_hot[:, s, j, :], ident[:, :])
                        last.then_inc(transposed, 1)

                    def count(i, s):
                        g = U * i + s
                        if exists(i, s, -SL):
                            pe.wait_ge(cnt_copied, g - SL + 1)
                            pe.wait_ge(col_added, g - SL + 1)
                        pe.wait_ge(place_ready, g + 1)
                        for j in range(T):
                            pe.wait_ge(hot_ready, T * g + j + 1)
                            for h in range(2):
                                last = nc.tensor.matmul(ps_cnt[:, s % SL, h, 0:WH * NB], l_hot[:, j, :],
                                                        k_hot[:, j, h * WH * NB:(h + 1) * WH * NB],
                                                        start=(j == 0), stop=(j == T - 1))
                            last.then_inc(cnt_done, 1)

                    def project(i, s):
                        g = U * i + s
                        pe.wait_ge(t_copied, g + 1)
                        pe.wait_ge(q_arrived[s % SL], 16 * turn(i, s))
                        if exists(i, s, -1):
                            pe.wait_ge(eq_used, g)
                        for c in range(T // 2):
                            nc.tensor.matmul(ps_eq[:, 0, 2 * c:2 * c + 2, :].rearrange("p j f -> p (j f)"), ea_T[:, c, :], we_diag[:, :],
                                             start=True, stop=True)
                        for j in range(T):
                            last = nc.tensor.matmul(ps_eq[:, 1, j, :], d_hot_T[:, j, :], q_win[:, s % SL, :], start=True, stop=True)
                        last.then_inc(eq_ready, 1)

                    transposes(0, 0)
                    project(0, 0)
                    transposes(0, 1)
                    count(0, 0)
                    pe.wait_ge(ones_ready, SL)

                    def body(i, s, _):
                        g = U * i + s
                        if exists(i, s, 1):
                            project(*at(i, s, 1))
                        if exists(i, s, 2):
                            transposes(*at(i, s, 2))
                        if exists(i, s, 1):
                            count(*at(i, s, 1))
                        pe.wait_ge(msg_ready, g + 1)
                        if exists(i, s, -1):
                            pe.wait_ge(sum_added, g)
                        for j in range(T):
                            last = nc.tensor.matmul(ps_sum[0:MSG, 0:W], msg[:, s % SL, j, :], d_hot[:, s, j, :],
                                                    start=(j == 0), stop=(j == T - 1))
                        last.then_inc(sum_done, 1)
                    steps(pe, body)
            e_ctx.close()
            edge_ctx.close()

            n_ctx = ExitStack()
            SCALE = 2.0 ** 9
            TOP = 14
            LAG = 3
            ON_ACT = 4
            WARMING = 16
            NORMED = 8.5
            EXP = 2.0 ** 23
            both = [sb(n_ctx, f"both{c}", [NP, NB, 2 * F]) for c in range(2)]
            x_again = both[1][:, :, 0:F]
            x1 = both[0][:, :, F:]
            y = both[0][:, :, 0:F]
            parts = [sb(n_ctx, "parts0", [NP, NB, 2, F], f16)[:, :, :, :],
                     sums_T[0:NP, 0:NB * F].bitcast(f16).rearrange("p (b c f) -> p b c f", c=2, f=F)]
            both_T = sums_T[:, NB * F:NB * F + 2 * BB * NP].rearrange("p (s w) -> p s w", s=2)
            w_rows = sb(n_ctx, "w_rows", [F, 2, 2 * F])
            w_stack = sb(n_ctx, "w_stack", [P, 2, F])
            w_abs = sb(n_ctx, "w_abs", [P, F])
            b_abs = sb(n_ctx, "b_abs", [P, F])
            b_scaled = sb(n_ctx, "b_scaled", [P, 2, F])
            ones = sb(n_ctx, "ones", [P, P])
            bound = sb(n_ctx, "bound", [P, F])
            top = sb(n_ctx, "top", [P, 1])
            expo = sb(n_ctx, "expo", [P, 1])
            power_i = sb(n_ctx, "power_i", [P, 1], i32)
            scale_i = sb(n_ctx, "scale_i", [P, 1], i32)
            rz = sb(n_ctx, "rz", [NP, NB, HEADS])
            rcnt = sb(n_ctx, "rcnt", [NP, NB])
            stats = sb(n_ctx, "stats", [NP, NB, 6])
            moments = sb(n_ctx, "moments", [NP, NB, 2])
            rstd = sb(n_ctx, "rstd", [NP, NB])
            shift = sb(n_ctx, "shift", [NP, NB])
            eps = sb(n_ctx, "eps", [NP, 2])
            eps_root = sb(n_ctx, "eps_root", [NP, 1])

            ps_a = pb(n_ctx, "ps_a", [P, 4, 512])
            ps_t = pb(n_ctx, "ps_t", [P, 2, 512])
            ps_g = pb(n_ctx, "ps_g", [P, 2, 512])

            b_arrived = sem("b_arrived")
            w_arrived, x_arrived = sem("w_arrived"), [sem("x_arrived0"), sem("x_arrived1")]
            ones_set = sem("ones_set")
            w_turned, w_stacked = sem("w_turned"), sem("w_stacked")
            abs_ready = sem("abs_ready")
            rows_summed = sem("rows_summed")
            scale_ready = sem("scale_ready")
            sums_turned = sem("sums_turned")
            attended = sem("attended")
            x_added = sem("x_added")
            var_ready = sem("var_ready")
            std_ready = sem("std_ready")
            rstd_ready = sem("rstd_ready")
            h_ready = [sem("h0_ready"), sem("h1_ready")]
            h_late = sem("h_late")
            hi_ready = sem("hi_ready")
            lo_ready = sem("lo_ready")
            agg_done = sem("agg_done")
            agg_used = sem("agg_used")
            mean_ready = sem("mean_ready")
            turned = sem("turned")
            turned_kept = sem("turned_kept")
            prod_done = sem("prod_done")
            prod_used = sem("prod_used")
            y_ready = sem("y_ready")
            chain = sem("node_chain")
            stored = sem("stored")

            def sums_bank(r):
                return ps_a[:, r, :] if r < 4 else ps_t[:, r - 4, :] if r < 6 else ps_g[:, 0, :]

            def input_ready(eng, c, r):
                if c == 0 and r >= ON_ACT:
                    eng.wait_ge(h_late, r - ON_ACT + 1)
                else:
                    eng.wait_ge(h_ready[c], r + 1)

            def blocks(r):
                return BB * r, min(BB, NB - BB * r)

            with nc.Block() as block:
                @block.sync
                def _(sp):
                    for s, (i0, i1) in enumerate(((0, 2 * BB), (2 * BB, NB))):
                        sp.dma_start(x_again[:, i0:i1, :], x.rearrange("(b p) f -> p b f", p=NP)[:, i0:i1, :]).then_inc(x_arrived[s], 16)
                    for c, (wl, wr) in enumerate([(Wl1, Wr1), (Wl2, Wr2)]):
                        sp.dma_start(w_rows[:, c, 0:F], wl).then_inc(w_arrived, 16)
                        sp.dma_start(w_rows[:, c, F:], wr).then_inc(w_arrived, 16)
                    for c, b in enumerate((b1, b2)):
                        sp.dma_start(bias[:, c, :], b.rearrange("(a f) -> a f", a=1).to_broadcast([P, F])).then_inc(b_arrived, 16)
                    for r in range(XG):
                        b0, k = blocks(r)
                        sp.wait_ge(y_ready, r + 1)
                        sp.dma_start(out.rearrange("(b p) f -> p b f", p=NP)[:, b0:b0 + k, :], y[:, b0:b0 + k, :]).then_inc(stored, 16)
                    sp.wait_ge(stored, 16 * XG)

                @block.tensor
                def _(pe):
                    for r in range(XG):
                        b0, k = blocks(r)
                        for b in range(b0, b0 + k):
                            last = nc.tensor.transpose(sums_bank(r)[0:NP, (b - b0) * MSG:(b - b0 + 1) * MSG],
                                                       sums_T[0:MSG, b * NP:(b + 1) * NP], ident[0:MSG, 0:MSG])
                        last.then_inc(sums_turned, 1)
                    for _ in range(WARMING):
                        nc.tensor.matmul(ps_g[:, 1, :], counts_T[0:NP, 0, 0:P], counts_T[0:NP, 0, 0:512], start=True, stop=True)
                    pe.wait_ge(w_arrived, 64)
                    for c in range(2):
                        last = nc.tensor.transpose(ps_g[:, 1, c * F:(c + 1) * F], w_rows[:, c, :], ident[0:F, 0:F])
                    last.then_inc(w_turned, 1)
                    pe.wait_ge(attended, 4)

                    def sum_edges(c, b, a0, a1, bank, column):
                        for a in range(a0, a1):
                            last = nc.tensor.matmul(ps_a[:, bank, column * 2 * F:(column + 1) * 2 * F],
                                                    counts_T[0:NP, a, b * NP:b * NP + P],
                                                    parts[c][:, a, :, :].rearrange("p c f -> p (c f)"),
                                                    start=(a == 0), stop=(a == NB - 1))
                        return last

                    def turn_round(c, r):
                        n = XG * c + r
                        b0, k = blocks(r)
                        pe.wait_ge(mean_ready, n + 1)
                        if n >= 2:
                            pe.wait_ge(turned_kept, n - 1)
                        for b in range(b0, b0 + k):
                            last = nc.tensor.transpose(ps_t[:, n % 2, (b - b0) * NP:(b - b0 + 1) * NP], both[c][:, b, :],
                                                       ident[0:NP, 0:NP])
                        last.then_inc(turned, 1)

                    def products(c, r):
                        n = XG * c + r
                        b0, k = blocks(r)
                        pe.wait_ge(turned_kept, n + 1)
                        if n >= 2:
                            pe.wait_ge(prod_used, n - 1)
                        else:
                            pe.wait_ge(scale_ready, 1)
                        for b in range(b0, b0 + k):
                            last = nc.tensor.matmul(ps_g[0:NP, n % 2, (b - b0) * F:(b - b0 + 1) * F],
                                                    both_T[:, n % 2, (b - b0) * NP:(b - b0 + 1) * NP], w_stack[:, c, :],
                                                    start=True, stop=True)
                        last.then_inc(prod_done, 1)

                    for c in range(2):
                        for ra in range(XG):
                            pe.wait_ge(lo_ready, XG * c + ra + 1)
                            for b in (2, 3, 0, 1):
                                if c and ra == 0 and b < 2:
                                    pe.wait_ge(agg_used, XG - 1 + b)
                                last = sum_edges(c, b, BB * ra, min(BB * ra + BB, NB), b, 0)
                            if c:
                                if ra == 0:
                                    products(0, XG - 2)
                                if ra == 1:
                                    turn_round(0, XG - 1)
                                if ra == 2:
                                    products(0, XG - 1)
                        last.then_inc(agg_done, 1)
                        if c == 0:
                            pe.wait_ge(ones_set, 3)
                            pe.wait_ge(abs_ready, 2)
                            nc.tensor.matmul(ps_g[:, 1, 0:F], ones[:, :], w_abs[:, :], start=True, stop=True).then_inc(rows_summed, 1)
                        for b in range(BB, NB):
                            r = b // BB
                            if b % BB == 0:
                                pe.wait_ge(agg_used, XG * c + max(1, r - 3))
                            last = sum_edges(c, b, 0, NB, (r - 1) % 4, b % BB)
                            if b % BB == BB - 1 or b == NB - 1:
                                last.then_inc(agg_done, 1)
                            if b % BB == 0:
                                turn_round(c, r - 1)
                            if b % BB == 1:
                                products(c, r - 1)
                    products(1, XG - 2)
                    turn_round(1, XG - 1)
                    products(1, XG - 1)

                @block.gpsimd
                def _(pool):
                    nc.gpsimd.memset(eps[:, 0:1], EPS / SCALE ** 2).then_inc(ones_set, 1)
                    nc.gpsimd.memset(eps[:, 1:2], EPS * SCALE ** 2).then_inc(ones_set, 1)
                    nc.gpsimd.memset(ones[:, :], 1.0).then_inc(ones_set, 1)

                    def low_parts(c, r):
                        b0, k = blocks(r)
                        pool.wait_ge(hi_ready, XG * c + r + 1)
                        nc.gpsimd.tensor_tensor(parts[c][:, b0:b0 + k, 1, :], both[c][:, b0:b0 + k, F:], parts[c][:, b0:b0 + k, 0, :],
                                                ALU.subtract).then_inc(lo_ready, 1)

                    for r in range(XG + LAG + 1):
                        if r < XG:
                            b0, k = blocks(r)
                            if r in (0, 2):
                                pool.wait_ge(x_arrived[r // 2], 16)
                            pool.wait_ge(attended, r + 1)
                            nc.gpsimd.tensor_tensor(x1[:, b0:b0 + k, :], x1[:, b0:b0 + k, :], x_again[:, b0:b0 + k, :],
                                                    ALU.add).then_inc(x_added, 1)
                        if r > LAG:
                            low_parts(0, r - LAG - 1)
                    for r in range(XG):
                        low_parts(1, r)

                @block.scalar
                def _(act):
                    def roots(n, r):
                        b0, k = blocks(r)
                        act.wait_ge(var_ready, n + 1)
                        c = n // XG
                        nc.scalar.activation(rstd[:, b0:b0 + k], moments[:, b0:b0 + k, 1], ACT.Sqrt, bias=eps[:, c:c + 1],
                                             scale=(SCALE ** -2, 1.0)[c]).then_inc(std_ready, 1)

                    def norm(n, h, r, ready):
                        b0, k = blocks(r)
                        act.wait_ge(rstd_ready, n + 1)
                        for b in range(b0, b0 + k):
                            last = nc.scalar.activation(h[:, b, :], h[:, b, :], ACT.Identity, bias=shift[:, b:b + 1], scale=rstd[:, b:b + 1])
                        last.then_inc(ready, 1)

                    def high_parts(c, r):
                        b0, k = blocks(r)
                        input_ready(act, c, r)
                        nc.scalar.activation(parts[c][:, b0:b0 + k, 0, :], both[c][:, b0:b0 + k, F:], ACT.Copy).then_inc(hi_ready, 1)

                    act.wait_ge(ones_set, 3)
                    nc.scalar.activation(eps_root[:, :], eps[:, 0:1], ACT.Sqrt)
                    roots(0, 0)
                    for r in range(1, XG + 1):
                        if r < XG:
                            roots(r, r)
                        if r <= ON_ACT:
                            norm(r - 1, x1, r - 1, h_ready[0])
                        high_parts(0, r - 1)
                    act.wait_ge(w_turned, 1)
                    nc.scalar.activation(w_stack[:, :, :].rearrange("p c f -> p (c f)"), ps_g[:, 1, 0:2 * F], ACT.Copy).then_inc(w_stacked, 1)
                    nc.scalar.activation(w_abs[:, :], ps_g[:, 1, 0:F], ACT.Abs).then_inc(abs_ready, 1)
                    act.wait_ge(b_arrived, 32)
                    nc.scalar.activation(b_abs[:, :], bias[:, 0, :], ACT.Abs).then_inc(abs_ready, 1)
                    for c in range(2):
                        for r in range(XG + 1):
                            if r < XG:
                                n = XG * c + r
                                w = blocks(r)[1] * NP
                                act.wait_ge(turned, n + 1)
                                if n >= 2:
                                    act.wait_ge(prod_done, n - 1)
                                nc.scalar.activation(both_T[:, n % 2, 0:w], ps_t[:, n % 2, 0:w], ACT.Copy).then_inc(turned_kept, 1)
                            if r and c == 0:
                                high_parts(1, r - 1)
                            if r and c == 1:
                                roots(XG + r - 1, r - 1)
                                norm(XG + r - 1, y, r - 1, y_ready)

                @block.vector
                def _(dve):
                    steps_done = [0]

                    def after(ins):
                        steps_done[0] += 1
                        ins.then_inc(chain, 1)
                        dve.wait_ge(chain, steps_done[0])

                    def wide(a, k, w):
                        return a.rearrange("p (b a) -> p b a", a=1).to_broadcast([NP, k, w])

                    def divisors(r0, banks, k):
                        n, b0 = banks.shape[1], BB * r0
                        dve.wait_ge(sums_turned, r0 + n)
                        sums = banks[0:NP, :, 0:k * MSG].rearrange("p q (b m) -> p q b m", m=MSG)
                        nc.vector.tensor_scalar(rcnt[:, b0:b0 + n * k].rearrange("p (q b) -> p q b", b=k), sums[:, :, :, F + HEADS],
                                                1.0, None, ALU.max)
                        z = rz[:, b0:b0 + n * k, :]
                        after(nc.vector.tensor_scalar(z.rearrange("p (q b) h -> p q b h", b=k), sums[:, :, :, F:F + HEADS], 1e-6, None, ALU.add))
                        after(nc.vector.reciprocal(z, z))

                    def attention(r):
                        b0, k = blocks(r)
                        if r == 0:
                            divisors(0, ps_a[:, :, :], BB)
                        if r == 4:
                            divisors(4, ps_t[:, :, :], BB)
                        if r == 6:
                            divisors(6, ps_g[:, 0:1, :], NB - 6 * BB)
                        sums = sums_bank(r)[0:NP, 0:k * MSG].rearrange("p (b m) -> p b m", m=MSG)
                        nc.vector.tensor_tensor(x1[:, b0:b0 + k, :].rearrange("p b (h f) -> p b h f", f=HD),
                                                sums[:, :, 0:F].rearrange("p b (h f) -> p b h f", f=HD),
                                                rz[:, b0:b0 + k, :].rearrange("p b (h a) -> p b h a", a=1).to_broadcast([NP, k, HEADS, HD]),
                                                ALU.mult).then_inc(attended, 1)

                    def measure(src_, r):
                        b0, k = blocks(r)
                        for b in range(b0, b0 + k):
                            last = nc.vector.bn_stats(stats[:, b, :], src_[:, b, :])
                        after(last)
                        for b in range(b0, b0 + k):
                            last = nc.vector.bn_aggr(moments[:, b, :], stats[:, b, :])
                        last.then_inc(var_ready, 1)

                    def invert(n, r):
                        b0, k = blocks(r)
                        dve.wait_ge(std_ready, n + 1)
                        after(nc.vector.reciprocal(rstd[:, b0:b0 + k], rstd[:, b0:b0 + k]))
                        nc.vector.scalar_tensor_tensor(out=shift[:, b0:b0 + k], in0=moments[:, b0:b0 + k, 0], scalar=-1.0,
                                                       in1=rstd[:, b0:b0 + k], op0=ALU.mult, op1=ALU.mult).then_inc(rstd_ready, 1)

                    for r in range(XG + LAG + 1):
                        if r < XG:
                            attention(r)
                        if LAG <= r < XG + LAG:
                            dve.wait_ge(x_added, r - LAG + 1)
                            measure(x1, r - LAG)
                        if r > LAG:
                            invert(r - LAG - 1, r - LAG - 1)
                        if r > LAG + ON_ACT:
                            dve.wait_ge(rstd_ready, r - LAG)
                            b0, k = blocks(r - LAG - 1)
                            for b in range(b0, b0 + k):
                                last = nc.vector.tensor_scalar(x1[:, b, :], x1[:, b, :], moments[:, b, 0:1], rstd[:, b:b + 1],
                                                               ALU.subtract, ALU.mult)
                            last.then_inc(h_late, 1)

                    after(nc.vector.reciprocal(rcnt[:, :], rcnt[:, :]))

                    def scales():
                        dve.wait_ge(rows_summed, 1)
                        dve.wait_ge(abs_ready, 2)
                        after(nc.vector.scalar_tensor_tensor(out=bound[:, :], in0=ps_g[:, 1, 0:F], scalar=NORMED, in1=b_abs[:, :],
                                                             op0=ALU.mult, op1=ALU.add))
                        after(nc.vector.reduce_max(top[:, :], bound[:, :], axis=X))
                        after(nc.vector.tensor_scalar(top[:, :], top[:, :], 1e-18, 1e30, ALU.max, ALU.min))
                        after(nc.vector.tensor_scalar(expo[:, :], top[:, 0:1].bitcast(i32), 1.0 / EXP, MAGIC, ALU.mult, ALU.add))
                        after(nc.vector.tensor_scalar(power_i[:, :], expo[:, :], -MAGIC, EXP, ALU.add, ALU.mult))
                        after(nc.vector.tensor_scalar(scale_i[:, :], power_i[:, :], -1.0, (2 * 127 + TOP) * EXP, ALU.mult, ALU.add))
                        dve.wait_ge(w_stacked, 1)
                        second, over = scale_i[:, 0:1].bitcast(f32), power_i[:, 0:1].bitcast(f32)
                        nc.vector.tensor_scalar(w_stack[:, 0, :], w_stack[:, 0, :], second, 1.0 / SCALE, ALU.mult, ALU.mult)
                        nc.vector.tensor_scalar(w_stack[:, 1, :], w_stack[:, 1, :], over, SCALE * 2.0 ** -TOP, ALU.mult, ALU.mult)
                        nc.vector.tensor_scalar(b_scaled[:, 0, :], bias[:, 0, :], second, None, ALU.mult)
                        after(nc.vector.tensor_scalar(b_scaled[:, 1, :], bias[:, 1, :], SCALE, None, ALU.mult))
                        nc.vector.nop().then_inc(scale_ready, 1)

                    def means(c, r):
                        n = XG * c + r
                        b0, k = blocks(r)
                        dve.wait_ge(agg_done, n + 1)
                        sums = ps_a[0:NP, :, 0:2 * F] if r == 0 else ps_a[0:NP, (r - 1) % 4, 0:k * 2 * F].rearrange("p (b w) -> p b w", w=2 * F)
                        mean = both[c][:, b0:b0 + k, 0:F]
                        nc.vector.reduce_sum(mean, sums.rearrange("p b (c f) -> p b f c", c=2), axis=X).then_inc(agg_used, 1)
                        dve.wait_ge(agg_used, n + 1)
                        nc.vector.tensor_tensor(mean, mean, wide(rcnt[:, b0:b0 + k], k, F), ALU.mult).then_inc(mean_ready, 1)

                    for c in range(2):
                        for r in range(XG + 1):
                            if r < XG:
                                means(c, r)
                            if r == 0:
                                if c == 0:
                                    scales()
                                continue
                            n = XG * c + r - 1
                            b0, k = blocks(r - 1)
                            h = (both[1][:, b0:b0 + k, F:], y[:, b0:b0 + k, :])[c]
                            dve.wait_ge(prod_done, n + 1)
                            nc.vector.tensor_tensor(h, ps_g[0:NP, n % 2, 0:k * F].rearrange("p (b f) -> p b f", f=F),
                                                    b_scaled[0:NP, c:c + 1, :].to_broadcast([NP, k, F]), ALU.add).then_inc(prod_used, 1)
                            dve.wait_ge(prod_used, n + 1)
                            if c == 0:
                                nc.vector.tensor_scalar(h, h, 0.0, None, ALU.max).then_inc(h_ready[1], 1)
                            else:
                                after(nc.vector.scalar_tensor_tensor(out=h, in0=h, scalar=0.0, in1=x1[:, b0:b0 + k, :],
                                                                     op0=ALU.max, op1=ALU.add))
                                measure(y, r - 1)
                                invert(n, r - 1)
            n_ctx.close()
            counts_ctx.close()


_INS = ["x", "src", "dst", "edge_attr_64", "L0_gnn_Wq", "L0_gnn_Wk", "L0_gnn_We", "L0_gnn_Wv", "L1_gnn_W_l1",
        "L1_gnn_b1", "L1_gnn_W_r1", "L1_gnn_W_l2", "L1_gnn_b2", "L1_gnn_W_r2"]


def kernel(**inputs):
    import numpy as np
    import concourse.bacc as bacc
    from concourse import mybir
    from concourse.bass_utils import run_bass_kernel_spmd as run

    nc = bacc.Bacc("TRN2", target_bir_lowering=False, num_devices=1)
    arrays, args = {}, []
    for name in _INS:
        a = np.ascontiguousarray(inputs[name])
        arrays[f"in_{name}"] = a
        args.append(nc.dram_tensor(f"in_{name}", a.shape, mybir.dt.from_np(a.dtype), kind="ExternalInput").ap())
    n, f = inputs["x"].shape
    args.append(nc.dram_tensor("out_0", (n, f), mybir.dt.float32, kind="ExternalOutput").ap())
    gnn_kernel(nc, *args)
    return run(nc, [arrays], core_ids=[0]).results[0]["out_0"]
```
